# Optimizing a Trainium2 kernel written in Bass

```python
import numpy as np
import jax
import jax.numpy as jnp

def _softmax(x, axis=-1):
    return jax.nn.softmax(x, axis=axis)

def _gelu(x):
    return jax.nn.gelu(x, approximate=True)

def _silu(x):
    return jax.nn.silu(x)

def _sigmoid(x):
    return jax.nn.sigmoid(x)

def _layernorm(x, axis=-1, eps=1e-05):
    m = jnp.mean(x, axis=axis, keepdims=True)
    v = jnp.var(x, axis=axis, keepdims=True)
    return (x - m) / jnp.sqrt(v + eps)

def _scatter_add(tgt, idx, src, axis=0):
    return tgt.at[idx].add(src)

def _segment_sum(src, seg, n):
    return jax.ops.segment_sum(src, seg, n)
kernel_name = 'mk_adj_preln_d1_adj_r2_907318'

def setup_inputs(seed: int=0):
    np.random.seed(seed)
    _w = jnp.asarray

    def _rec_inputs():
        import jax
        import jax.numpy as jnp
        _gk = jax.random.key(seed)
        x = -0.0002928 + 1 * jax.random.normal(jax.random.fold_in(_gk, 1), (8192, 256), jnp.float32)
        _w = (1.0 + jnp.arange(8192, dtype=jnp.float32)) ** (-0.5)
        _w = _w / _w.mean()
        _pij = jnp.clip(0.000244141 * _w[:, None] * _w[None, :], 0.0, 1.0)
        _a = jax.random.uniform(jax.random.fold_in(_gk, 2), (8192, 8192)) < _pij
        adj = _a.astype(jnp.int32)
        return (x, adj)
    x, adj = _rec_inputs()

    def _L0_gnn_setup():
        import jax, jax.numpy as jnp
        import numpy as np
        N, D_IN, D_OUT = (4096, 256, 256)
        key = jax.random.key(seed)
        ks = jax.random.split(key, 8)
        scale_in = 1.0 / np.sqrt(D_IN)
        scale_cat = 1.0 / np.sqrt(2 * D_OUT)
        return {'x': jax.random.normal(ks[0], (N, D_IN), dtype=jnp.float32), 'adj': jax.random.randint(ks[1], (N, N), 0, 2, dtype=jnp.int32), 'W_self': jax.random.uniform(ks[2], (D_IN, D_OUT), jnp.float32, -scale_in, scale_in), 'b_self': jax.random.uniform(ks[3], (D_OUT,), jnp.float32, -scale_in, scale_in), 'W_nb': jax.random.uniform(ks[4], (D_IN, D_OUT), jnp.float32, -scale_in, scale_in), 'b_nb': jax.random.uniform(ks[5], (D_OUT,), jnp.float32, -scale_in, scale_in), 'W_comb': jax.random.uniform(ks[6], (2 * D_OUT, D_OUT), jnp.float32, -scale_cat, scale_cat), 'b_comb': jax.random.uniform(ks[7], (D_OUT,), jnp.float32, -scale_cat, scale_cat)}
    _L0_gnn_all = _L0_gnn_setup()
    _L0_gnn_in = {k: v for k, v in _L0_gnn_all.items() if k in ('W_self', 'b_self', 'W_nb', 'b_nb', 'W_comb', 'b_comb')}
    del _L0_gnn_all
    return {'x': x, 'adj': adj, 'L0_gnn_W_self': _L0_gnn_in['W_self'], 'L0_gnn_b_self': _L0_gnn_in['b_self'], 'L0_gnn_W_nb': _L0_gnn_in['W_nb'], 'L0_gnn_b_nb': _L0_gnn_in['b_nb'], 'L0_gnn_W_comb': _L0_gnn_in['W_comb'], 'L0_gnn_b_comb': _L0_gnn_in['b_comb']}

def reference(x, adj, L0_gnn_W_self, L0_gnn_b_self, L0_gnn_W_nb, L0_gnn_b_nb, L0_gnn_W_comb, L0_gnn_b_comb):
    import jax
    import jax.numpy as jnp

    def _L0_gnn_ref(x, adj, W_self, b_self, W_nb, b_nb, W_comb, b_comb):
        import jax, jax.numpy as jnp
        import numpy as np
        N, D_IN, D_OUT = (4096, 256, 256)
        mask = (adj > 0).astype(x.dtype)
        deg = jnp.sum(mask, axis=1, keepdims=True)
        agg = mask @ x / jnp.maximum(deg, 1.0)
        self_f = x @ W_self + b_self
        nb_f = agg @ W_nb + b_nb
        combined = jnp.concatenate([self_f, nb_f], axis=-1)
        out = combined @ W_comb + b_comb
        return jax.nn.relu(out)
    h = jnp.maximum(_layernorm(x, axis=-1), 0.0)
    x = x + _L0_gnn_ref(h, adj, L0_gnn_W_self, L0_gnn_b_self, L0_gnn_W_nb, L0_gnn_b_nb, L0_gnn_W_comb, L0_gnn_b_comb)
    return x

_drawn_inputs = setup_inputs


def setup_inputs(seed=0):
    import zlib

    import numpy as np

    out = dict(_drawn_inputs(seed))
    spreads = {}
    factors = {'L0_gnn_b_self': 5.996, 'L0_gnn_b_nb': 5.291, 'L0_gnn_b_comb': 3.152}
    for name, (base, spread) in spreads.items():
        noise = np.random.default_rng([zlib.crc32(name.encode()), seed]).standard_normal(out[name].shape)
        drawn = base * np.exp(spread * noise) if base else spread * noise
        out[name] = jnp.asarray(drawn.astype(out[name].dtype))
    for name, factor in factors.items():
        out[name] = (out[name] * factor).astype(out[name].dtype)
    return out
```

```python
from contextlib import ExitStack

import concourse.bass as bass
from concourse import mybir

F32 = mybir.dt.float32
F16 = mybir.dt.float16
FP8 = mybir.dt.float8e4
I32 = mybir.dt.int32
U32 = mybir.dt.uint32
U8 = mybir.dt.uint8
ALU = mybir.AluOpType
ACT = mybir.ActivationFunctionType

P = 128
QUAD = 4
LANE = P // QUAD
SUB = 4
SCALE = 2.0 ** 11
ONE_BYTE = 64
EDGE = 2.0
EPS = 1e-5

STAGES = 4
MASKS = 4
XRING = 4
DONE = 16


def graph_layer(nc, x, adj, w_self, b_self, w_nb, b_nb, w_comb, b_comb, out):
    N, D = x.shape
    HALVES = D // P
    SPAN = N // QUAD
    WORDS = SPAN // SUB
    CHUNKS = SPAN // (LANE * SUB)
    ROWS = N // CHUNKS
    GROUPS = ROWS // LANE
    TILES = N // P
    PAIRS = (CHUNKS - 2) // 2
    assert D == 2 * P and ROWS == 512 and GROUPS == 16 and CHUNKS % 2 == 0
    assert GROUPS % STAGES == 0 and GROUPS % MASKS == 0 and CHUNKS % XRING == 0

    adj_v = adj.rearrange("(a c l s) (b f) -> a c l s b f", a=QUAD, c=CHUNKS, l=LANE, s=SUB, b=QUAD)
    x_v = x.rearrange("(a c l s) d -> a c l (s d)", a=QUAD, c=CHUNKS, l=LANE, s=SUB)
    out_v = out.rearrange("(a c l s) d -> a c l (s d)", a=QUAD, c=CHUNKS, l=LANE, s=SUB)

    with ExitStack() as ctx:
        def sb(name, shape, dt):
            return ctx.enter_context(nc.sbuf_tensor(name, shape, dt))

        def sem(name):
            return ctx.enter_context(nc.semaphore(name))

        mask_t = sb("mask_t", [P, 2, CHUNKS, GROUPS, LANE], U32)
        h16 = sb("h16", [P, 2, TILES, D], F16)
        stage = sb("stage", [P, STAGES, SPAN], I32)
        mask = sb("mask", [P, MASKS, SPAN], U8)
        counted = sb("counted", [P, 2, SPAN], U8)
        x_again = sb("x_again", [P, 2, SUB, D], F32)
        sum_t = sb("sum_t", [P, HALVES, ROWS], F32)
        h_t = sb("h_t", [P, HALVES, ROWS], F32)
        w1 = sb("w1", [P, HALVES, D], F32)
        w2 = sb("w2", [P, HALVES, D], F32)
        c_row = sb("c_row", [P, D], F32)
        ident16 = sb("ident16", [P, P], F16)
        fold = sb("fold", [P, QUAD, P], F16)
        layer = sb("layer", [P, 2, D], F32)
        deg_part = sb("deg_part", [P, 2, GROUPS], F32)
        deg16 = sb("deg16", [P, GROUPS], F16)
        deg = sb("deg", [P, SUB], F32)
        rdeg = sb("rdeg", [P, SUB], F32)

        spare = mask_t[:, 1, :, :, :].rearrange("p c g l -> p (c g l)").bitcast(F32)
        cursor = [0]

        def early(n):
            cursor[0] += n
            assert cursor[0] <= CHUNKS * ROWS
            return spare[:, cursor[0] - n:cursor[0]]

        x_ring = early(XRING * SUB * D).rearrange("p (e s d) -> p e s d", e=XRING, s=SUB)
        ws = early(HALVES * D).rearrange("p (h n) -> p h n", h=HALVES)
        wn = early(HALVES * D).rearrange("p (h n) -> p h n", h=HALVES)
        wc = early(2 * HALVES * D).rearrange("p (h n) -> p h n", h=2 * HALVES)
        ws_t = early(HALVES * D).rearrange("p (m k) -> p m k", m=HALVES)
        wn_t = early(HALVES * D).rearrange("p (m k) -> p m k", m=HALVES)
        ident = early(P)
        ones = early(P)
        b_cols = early(2 * HALVES)
        b_wide = early(2 * HALVES * P).rearrange("p (h m) -> p h m", h=2 * HALVES)
        bc_row = layer[:, 0, :]
        stats = early(2 * SUB * 6).rearrange("p (e s k) -> p e s k", e=2, s=SUB)
        mean_var = early(2 * SUB * 2).rearrange("p (e s k) -> p e s k", e=2, s=SUB)
        var_s = early(2 * SUB).rearrange("p (e s) -> p e s", e=2)
        rstd = early(2 * SUB).rearrange("p (e s) -> p e s", e=2)
        power = early(SUB)

        banks = [ctx.enter_context(nc.psum_tensor(f"bank{n}", [P, ROWS], F32)) for n in range(8)]
        sum_ps = [banks[0:2], banks[2:4]]
        h_ps = banks[4:6]
        out_ps = [b[:, :].rearrange("p (w n) -> p w n", w=2) for b in banks[6:8]]

        stage_full = [sem(f"stage_full{n}") for n in range(STAGES)]
        masked = sem("masked")
        transposed = sem("transposed")
        counted_rows = sem("counted_rows")
        x_full = [sem(f"x_full{n}") for n in range(XRING)]
        stats_done = sem("stats_done")
        aggr_done = sem("aggr_done")
        var_ready = sem("var_ready")
        rstd_ready = sem("rstd_ready")
        normed = sem("normed")
        clipped = sem("clipped")
        high_ready = sem("high_ready")
        low_ready = sem("low_ready")
        w_loaded = sem("w_loaded")
        zeroed = sem("zeroed")
        ident_ready = sem("ident_ready")
        fold_ready = sem("fold_ready")
        wide_ready = sem("wide_ready")
        w_turned = sem("w_turned")
        wt_ready = sem("wt_ready")
        w_product = sem("w_product")
        w_ready = sem("w_ready")
        main_done = sem("main_done")
        sum_copied = sem("sum_copied")
        h_turned = sem("h_turned")
        h_copied = sem("h_copied")
        deg16_ready = sem("deg16_ready")
        deg_summed = sem("deg_summed")
        deg_clamped = sem("deg_clamped")
        rdeg_ready = sem("rdeg_ready")
        projected = sem("projected")
        out_read = sem("out_read")
        added = sem("added")
        x_again_full = [sem(f"x_again_full{n}") for n in range(2)]
        out_ready = sem("out_ready")
        stored = sem("stored")

        block = ctx.enter_context(nc.Block())

        def mask_words(n_slot):
            return mask[:, n_slot, :].bitcast(U32)

        @block.sync
        def _(sp):
            def load_group(s, g):
                sub, a = divmod(g, QUAD)
                for q in range(QUAD):
                    sp.dma_start(stage[LANE * q:LANE * (q + 1), g % STAGES, :],
                                 adj_v[a, s, :, sub, q, :]).then_inc(stage_full[g % STAGES], DONE)

            def load_x(dst, s, q, signal):
                sp.dma_start(dst[LANE * q:LANE * (q + 1), :], x_v[q, s, :, :]).then_inc(signal, DONE)

            for e in range(CHUNKS):
                if e >= XRING:
                    sp.wait_ge(low_ready, e - XRING + 1)
                for q in range(QUAD):
                    load_x(x_ring[:, e % XRING, :, :].rearrange("p s d -> p (s d)"), e, q, x_full[e % XRING])
                if e >= STAGES:
                    sp.wait_ge(masked, e - STAGES + 1)
                load_group(0, e)

            def load_chunk(s, g0, g1):
                for g in range(g0, g1):
                    sp.wait_ge(masked, s * GROUPS + (g - STAGES + 1))
                    load_group(s, g)

            def reload_x(s, parity, first=False):
                if not first:
                    sp.wait_ge(stored, (s - 1) * (QUAD * DONE))
                for q in range(QUAD):
                    load_x(x_again[:, parity, :, :].rearrange("p s d -> p (s d)"), s, q, x_again_full[parity])

            def store(s, parity):
                sp.wait_ge(out_ready, s * SUB + SUB)
                for q in range(QUAD):
                    sp.dma_start(out_v[q, s, :, :],
                                 x_again[LANE * q:LANE * (q + 1), parity, :, :].rearrange("p s d -> p (s d)")
                                 ).then_inc(stored, DONE)

            load_chunk(1, 0, GROUPS)
            reload_x(0, 0, first=True)
            reload_x(1, 1, first=True)
            with sp.Fori(0, PAIRS) as k:
                for par in range(2):
                    s = k * 2 + (2 + par)
                    load_chunk(s, 0, GROUPS)
                    store(k * 2 + par, par)
                    reload_x(k * 2 + (2 + par), par)
            store(CHUNKS - 2, 0)
            store(CHUNKS - 1, 1)
            sp.wait_ge(stored, CHUNKS * QUAD * DONE)

        @block.gpsimd
        def _(pool):
            pool.memset(ident, 0.0).then_inc(zeroed, 1)
            pool.memset(ones, 1.0).then_inc(zeroed, 1)
            pool.memset(power, -0.5).then_inc(zeroed, 1)
            pool.memset(fold[:, :, :], 0.0).then_inc(zeroed, 1)
            pool.wait_ge(zeroed, 4)
            pool.affine_select(out=ident, in_=ident, compare_op=ALU.not_equal, fill=1.0, base=0,
                               pattern=[[-1, P]], channel_multiplier=1).then_inc(ident_ready, 1)

            def rstd_of(e, slot):
                pool.wait_ge(aggr_done, (e + 1) * SUB)
                pool.tensor_scalar(var_s[:, slot, :], mean_var[:, slot, :, 1], EPS, SCALE ** -2,
                                   ALU.add, ALU.mult).then_inc(var_ready, 1)
                pool.wait_ge(var_ready, e + 1)
                pool.tensor_tensor(rstd[:, slot, :], var_s[:, slot, :], power, ALU.pow).then_inc(rstd_ready, 1)

            def remainder(e, slot, tiles):
                pool.wait_ge(high_ready, e + 1)
                pool.tensor_tensor(h16[:, 1, tiles, :], x_ring[:, slot, :, :], h16[:, 0, tiles, :],
                                   ALU.subtract).then_inc(low_ready, 1)

            rstd_of(0, 0)
            for e in range(CHUNKS):
                if e + 1 < CHUNKS:
                    rstd_of(e + 1, (e + 1) % 2)
                remainder(e, e % XRING, slice(SUB * e, SUB * (e + 1)))

        @block.scalar
        def _(act):
            act.dma_start(wc, w_comb.rearrange("(h p) n -> p h n", p=P)).then_inc(w_loaded, DONE)
            act.dma_start(ws, w_self.rearrange("(h p) n -> p h n", p=P)).then_inc(w_loaded, DONE)
            act.dma_start(wn, w_nb.rearrange("(h p) n -> p h n", p=P)).then_inc(w_loaded, DONE)
            act.dma_start(bc_row, b_comb.rearrange("(a n) -> a n", a=1).partition_broadcast(P)).then_inc(w_loaded, DONE)
            act.dma_start(b_cols[:, 0:HALVES], b_self.rearrange("(h p) -> p h", p=P),
                          allow_slow_non_contiguous=True).then_inc(w_loaded, DONE)
            act.dma_start(b_cols[:, HALVES:2 * HALVES], b_nb.rearrange("(h p) -> p h", p=P),
                          allow_slow_non_contiguous=True).then_inc(w_loaded, DONE)

            act.wait_ge(w_loaded, 6 * DONE)
            act.wait_ge(zeroed, 4)
            for j in range(2 * HALVES):
                act.activation(b_wide[:, j, :], ones, ACT.Copy, scale=b_cols[:, j:j + 1]).then_inc(wide_ready, 1)

            act.wait_ge(w_turned, 1)
            act.activation(ws_t.rearrange("p m k -> p (m k)"), banks[4][:, :], ACT.Copy).then_inc(wt_ready, 1)
            act.activation(wn_t.rearrange("p m k -> p (m k)"), banks[5][:, :], ACT.Copy).then_inc(wt_ready, 1)

            act.wait_ge(w_product, 1)
            act.activation(w1[:, :, :].rearrange("p h n -> p (h n)"), banks[6][:, :], ACT.Copy).then_inc(w_ready, 1)
            act.activation(w2[:, :, :].rearrange("p h n -> p (h n)"), banks[7][:, :], ACT.Copy).then_inc(w_ready, 1)

            def count(s, g, parity):
                act.wait_ge(masked, s * GROUPS + (g + 1))
                if not (isinstance(s, int) and s == 0 and g < 2):
                    act.wait_ge(counted_rows, s * GROUPS + (g - 1))
                act.activation(counted[:, g % 2, :], mask[:, g % MASKS, :], ACT.Copy,
                               accum_out=deg_part[:, parity, g:g + 1]).then_inc(counted_rows, 1)

            for e in range(CHUNKS):
                act.wait_ge(normed, SUB * (e + 1))
                act.activation(x_ring[:, e % XRING, :, :], x_ring[:, e % XRING, :, :], ACT.Relu).then_inc(clipped, 1)
                act.wait_ge(clipped, e + 1)
                act.activation(h16[:, 0, SUB * e:SUB * (e + 1), :], x_ring[:, e % XRING, :, :],
                               ACT.Copy).then_inc(high_ready, 1)
                count(0, e, 0)

            def chunk_counts(s, parity, wait):
                if wait:
                    act.wait_ge(deg16_ready, s - 1)
                for g in range(GROUPS):
                    count(s, g, parity)

            def drain(s, parity, first=False):
                act.wait_ge(main_done, s + 1)
                if not first:
                    act.wait_ge(projected, s * SUB)
                for half in range(HALVES):
                    act.activation(sum_t[:, half, :], sum_ps[parity][half][:, :], ACT.Copy).then_inc(sum_copied, 1)
                act.wait_ge(h_turned, s + 1)
                for half in range(HALVES):
                    act.activation(h_t[:, half, :], h_ps[half][:, :], ACT.Copy).then_inc(h_copied, 1)

            chunk_counts(1, 1, False)
            drain(0, 0, first=True)
            chunk_counts(2, 0, True)
            with act.Fori(0, PAIRS - 1) as k:
                for par in range(2):
                    drain(k * 2 + (1 + par), 1 - par)
                    chunk_counts(k * 2 + (3 + par), 1 - par, True)
            drain(CHUNKS - 3, 1)
            chunk_counts(CHUNKS - 1, 1, True)
            drain(CHUNKS - 2, 0)
            drain(CHUNKS - 1, 1)

        @block.tensor
        def _(pe):
            pe.wait_ge(w_loaded, 6 * DONE)
            pe.wait_ge(ident_ready, 2)
            for w, bank in ((ws, banks[4]), (wn, banks[5])):
                for m in range(HALVES):
                    for kk in range(HALVES):
                        at = m * D + kk * P
                        mm = pe.transpose(bank[:, at:at + P], w[:, kk, m * P:(m + 1) * P], ident)
            mm.then_inc(w_turned, 1)
            pe.wait_ge(wt_ready, 2)
            for n, (w_t, bank) in enumerate(((ws_t, banks[6]), (wn_t, banks[7]))):
                for kk in range(HALVES):
                    for m in range(HALVES):
                        pe.matmul(bank[:, kk * D:(kk + 1) * D], w_t[:, m, kk * P:(kk + 1) * P],
                                  wc[:, n * HALVES + m, :], start=(m == 0), stop=(m == HALVES - 1))
            pe.wait_ge(wide_ready, 2 * HALVES)
            for m in range(2 * HALVES):
                mm = pe.matmul(banks[3][:, 0:D], b_wide[:, m, :], wc[:, m, :],
                               start=(m == 0), stop=(m == 2 * HALVES - 1))
            mm.then_inc(w_product, 1)

            def sum_step(parity, e, sub):
                words = mask_t[:, parity, e, :, :].rearrange("p g l -> p (g l)").bitcast(FP8)
                rhs = words.rearrange("p (i s) -> p i s", s=SUB)[:, :, sub]
                for half in range(HALVES):
                    for part in range(2):
                        mm = pe.matmul(sum_ps[parity][half][:, :],
                                       h16[:, part, SUB * e + sub, half * P:(half + 1) * P], rhs,
                                       start=(e == 0 and sub == 0 and part == 0),
                                       stop=(e == CHUNKS - 1 and sub == SUB - 1 and part == 1))
                return mm

            def turn_h(s, first=False):
                if not first:
                    pe.wait_ge(h_copied, s * HALVES)
                for half in range(HALVES):
                    for sub in range(SUB):
                        for part in range(2):
                            lhs = h16[:, part, bass.ds(s * SUB + sub, 1), half * P:(half + 1) * P]
                            mm = pe.matmul(h_ps[half][:, sub * P:(sub + 1) * P],
                                           lhs.rearrange("p o d -> p (o d)"), ident16[:, :],
                                           start=(part == 0), stop=(part == 1))
                mm.then_inc(h_turned, 1)

            def sum_degrees(s, parity, first=False):
                pe.wait_ge(sum_copied, s * HALVES + HALVES)
                if first:
                    pe.wait_ge(fold_ready, QUAD * QUAD)
                pe.wait_ge(deg16_ready, s + 1)
                for a in range(QUAD):
                    mm = pe.matmul(sum_ps[parity][0][:, 0:SUB], fold[:, a, :], deg16[:, a:GROUPS:QUAD],
                                   start=(a == 0), stop=(a == QUAD - 1))
                mm.then_inc(deg_summed, 1)

            def project(s, sub, first=False):
                if sub == 0:
                    pe.wait_ge(h_copied, s * HALVES + HALVES)
                if not (first and sub < 2):
                    pe.wait_ge(out_read, s * SUB + (sub - 1))
                rows = slice(sub * P, (sub + 1) * P)
                for n, (src, w) in enumerate(((h_t, w1), (sum_t, w2))):
                    for half in range(HALVES):
                        mm = pe.matmul(out_ps[sub % 2][:, n, :], src[:, half, rows], w[:, half, :],
                                       start=(half == 0), stop=(half == HALVES - 1))
                mm.then_inc(projected, 1)

            def chunk(s, parity, before=None, first=False):
                pe.wait_ge(transposed, s * GROUPS + GROUPS)
                if first:
                    pe.wait_ge(w_ready, 3)
                elif before is not None:
                    pe.wait_ge(rdeg_ready, s - 1)
                if before is not None:
                    turn_h(before, first)
                for e in range(CHUNKS):
                    if before is None:
                        pe.wait_ge(low_ready, e + 1)
                    for sub in range(SUB):
                        mm = sum_step(parity, e, sub)
                        if before is None:
                            continue
                        at = e * SUB + sub
                        if at == 7:
                            sum_degrees(before, 1 - parity, first)
                        if at in (11, 19, 27, 35):
                            project(before, (at - 11) // 8, first)
                mm.then_inc(main_done, 1)

            chunk(0, 0)
            chunk(1, 1, before=0, first=True)
            with pe.Fori(0, PAIRS) as k:
                for par in range(2):
                    chunk(k * 2 + (2 + par), par, before=k * 2 + (1 + par))
            last = CHUNKS - 1
            turn_h(last)
            sum_degrees(last, last % 2)
            for sub in range(SUB):
                project(last, sub)

        @block.vector
        def _(dve):
            def form_mask(s, g):
                dve.wait_ge(stage_full[g % STAGES],
                            (s * (GROUPS // STAGES) + (g // STAGES + 1)) * (QUAD * DONE))
                if not (isinstance(s, int) and s == 0 and g < MASKS):
                    dve.wait_ge(counted_rows, s * GROUPS + (g - MASKS + 1))
                    dve.wait_ge(transposed, s * GROUPS + (g - MASKS + 1))
                dve.tensor_scalar(mask[:, g % MASKS, :], stage[:, g % STAGES, :], 0.0, float(ONE_BYTE),
                                  ALU.is_gt, ALU.mult).then_inc(masked, 1)

            def turn_mask(s, g, parity):
                dve.wait_ge(masked, s * GROUPS + (g + 1))
                src = mask_words(g % MASKS).rearrange("p (c l) -> p c l", l=LANE)
                dve.transpose(mask_t[:, parity, :, g, :], src).then_inc(transposed, 1)

            def stats_of(e):
                dve.wait_ge(x_full[e % XRING], (e // XRING + 1) * QUAD * DONE)
                for sub in range(SUB):
                    dve.bn_stats(stats[:, e % 2, sub, :], x_ring[:, e % XRING, sub, :]).then_inc(stats_done, 1)
                dve.wait_ge(stats_done, (e + 1) * SUB)
                if e >= 2:
                    dve.wait_ge(rstd_ready, e - 1)
                for sub in range(SUB):
                    dve.bn_aggr(mean_var[:, e % 2, sub, :], stats[:, e % 2, sub, :]).then_inc(aggr_done, 1)

            def normalise(e):
                dve.wait_ge(rstd_ready, e + 1)
                for sub in range(SUB):
                    t = x_ring[:, e % XRING, sub, :]
                    dve.tensor_scalar(t, t, mean_var[:, e % 2, sub, 0:1], rstd[:, e % 2, sub:sub + 1],
                                      ALU.subtract, ALU.mult).then_inc(normed, 1)

            def pack(s, parity, first=False):
                dve.wait_ge(counted_rows, s * GROUPS + GROUPS)
                if not first:
                    dve.wait_ge(deg_summed, s)
                dve.tensor_scalar(deg16[:, :], deg_part[:, parity, :], 1.0 / ONE_BYTE, None, ALU.mult).then_inc(deg16_ready, 1)

            def invert_degrees(s, parity):
                dve.wait_ge(deg_summed, s + 1)
                dve.tensor_scalar(deg[:, :], sum_ps[parity][0][:, 0:SUB], 1.0, EDGE * SCALE, ALU.max, ALU.mult
                                  ).then_inc(deg_clamped, 1)
                dve.wait_ge(deg_clamped, s + 1)
                dve.reciprocal(rdeg[:, :], deg[:, :]).then_inc(rdeg_ready, 1)

            def finish(pair, parity, sub):
                s = pair * 2 + parity
                dve.wait_ge(projected, s * SUB + (sub + 1))
                if sub == 0:
                    dve.wait_ge(rdeg_ready, s + 1)
                    dve.wait_ge(x_again_full[parity], (pair + 1) * (QUAD * DONE))
                y = layer[:, sub % 2, :]
                xa = x_again[:, parity, sub, :]
                dve.scalar_tensor_tensor(y, out_ps[sub % 2][:, 1, :], rdeg[:, sub:sub + 1], c_row[:, :],
                                         ALU.mult, ALU.add).then_inc(added, 1)
                dve.wait_ge(added, s * SUB + (sub + 1))
                dve.scalar_tensor_tensor(y, out_ps[sub % 2][:, 0, :], 1.0 / SCALE, y,
                                         ALU.mult, ALU.add).then_inc(out_read, 1)
                dve.wait_ge(out_read, s * SUB + (sub + 1))
                dve.scalar_tensor_tensor(xa, y, 0.0, xa, ALU.max, ALU.add).then_inc(out_ready, 1)

            dve.wait_ge(ident_ready, 1)
            dve.tensor_copy(ident16[:, :], ident).then_inc(ident_ready, 1)
            for q in range(QUAD):
                rows = slice(LANE * q, LANE * (q + 1))
                for a in range(QUAD):
                    dve.tensor_copy(fold[rows, a, LANE * a:LANE * (a + 1)], ident[rows, rows]
                                    ).then_inc(fold_ready, 1)

            for e in range(CHUNKS):
                stats_of(e)
                form_mask(0, e)
                normalise(e)
                turn_mask(0, e, 0)

            dve.wait_ge(w_product, 1)
            dve.tensor_tensor(c_row[:, :], banks[3][:, 0:D], bc_row, ALU.add).then_inc(w_ready, 1)

            for g in range(GROUPS):
                form_mask(1, g)
                if g == 0:
                    dve.wait_ge(low_ready, CHUNKS)
                    dve.wait_ge(w_ready, 3)
                else:
                    turn_mask(1, g - 1, 1)
            turn_mask(1, GROUPS - 1, 1)
            pack(0, 0, first=True)

            with dve.Fori(1, PAIRS + 1) as k:
                for par in range(2):
                    s = k * 2 + par
                    for g in range(GROUPS):
                        form_mask(s, g)
                        if g == 0:
                            dve.wait_ge(main_done, s - 1)
                        else:
                            turn_mask(s, g - 1, par)
                        if g == 3:
                            invert_degrees(s - 2, par)
                            pack(s - 1, 1 - par)
                        if g in (5, 7, 9, 11):
                            finish(k - 1, par, (g - 5) // 2)
                    turn_mask(s, GROUPS - 1, par)
            last = CHUNKS - 1
            invert_degrees(last - 1, 0)
            pack(last, 1)
            for sub in range(SUB):
                finish(last // 2, 0, sub)
            invert_degrees(last, 1)
            for sub in range(SUB):
                finish(last // 2, 1, sub)


_INS = ["x", "adj", "L0_gnn_W_self", "L0_gnn_b_self", "L0_gnn_W_nb", "L0_gnn_b_nb", "L0_gnn_W_comb", "L0_gnn_b_comb"]


def kernel(**inputs):
    import numpy as np
    import concourse.bacc as bacc
    from concourse.bass_utils import run_bass_kernel_spmd

    nc = bacc.Bacc("TRN2", target_bir_lowering=False, num_devices=1)
    arrays, args = {}, []
    for name in _INS:
        a = np.ascontiguousarray(inputs[name])
        arrays[f"in_{name}_dram"] = a
        args.append(nc.dram_tensor(f"in_{name}_dram", a.shape, mybir.dt.from_np(a.dtype), kind="ExternalInput").ap())
    shape = arrays["in_x_dram"].shape
    out = nc.dram_tensor("out_0_dram", shape, F32, kind="ExternalOutput").ap()
    graph_layer(nc, *args, out)
    r = run_bass_kernel_spmd(nc, [arrays], core_ids=[0])
    return r.results[0]["out_0_dram"]
```

```python
from contextlib import ExitStack

import concourse.bass as bass
from concourse import mybir

F32 = mybir.dt.float32
F16 = mybir.dt.float16
FP8 = mybir.dt.float8e4
I32 = mybir.dt.int32
U32 = mybir.dt.uint32
U8 = mybir.dt.uint8
ALU = mybir.AluOpType
ACT = mybir.ActivationFunctionType

P = 128
QUAD = 4
LANE = P // QUAD
SUB = 4
SCALE = 2.0 ** 11
ONE_BYTE = 64
EDGE = 2.0
EPS = 1e-5

STAGES = 4
MASKS = 8
XRING = 8
DONE = 16

GROUPS_OF_PAIR = [[0], [1], [2, 3], [4], [5], [6, 7], [], []]
FIRST_GROUPS = sum(map(len, GROUPS_OF_PAIR))


NORM_ON_VECTOR = (5, 11, 14, 15)
LOW_ON_VECTOR = (5, 9, 11, 14, 15)
COUNTS_BEFORE = {4: 0, 6: 1, 12: 2}


def up_to(e, some):
    return sum(i <= e for i in some)


def graph_layer(nc, x, adj, w_self, b_self, w_nb, b_nb, w_comb, b_comb, out):
    N, D = x.shape
    HALVES = D // P
    SPAN = N // QUAD
    WORDS = SPAN // SUB
    CHUNKS = SPAN // (LANE * SUB)
    ROWS = N // CHUNKS
    GROUPS = ROWS // LANE
    TILES = N // P
    PAIRS = (CHUNKS - 2) // 2
    assert D == 2 * P and ROWS == 512 and GROUPS == 16 and CHUNKS % 2 == 0
    assert GROUPS % STAGES == 0 and GROUPS % MASKS == 0 and CHUNKS % XRING == 0

    adj_v = adj.rearrange("(a c l s) (b f) -> a c l s b f", a=QUAD, c=CHUNKS, l=LANE, s=SUB, b=QUAD)
    x_v = x.rearrange("(a c l s) d -> a c l (s d)", a=QUAD, c=CHUNKS, l=LANE, s=SUB)
    out_v = out.rearrange("(a c l s) d -> a c l (s d)", a=QUAD, c=CHUNKS, l=LANE, s=SUB)

    with ExitStack() as ctx:
        def sb(name, shape, dt):
            return ctx.enter_context(nc.sbuf_tensor(name, shape, dt))

        def sem(name):
            return ctx.enter_context(nc.semaphore(name))

        mask_t = sb("mask_t", [P, 2, CHUNKS, GROUPS, LANE], U32)
        h16 = sb("h16", [P, 2, TILES, D], F16)
        stage = sb("stage", [P, STAGES, SPAN], I32)
        mask = sb("mask", [P, MASKS, SPAN], U8)
        counted = sb("counted", [P, 2, SPAN], U8)
        x_again = sb("x_again", [P, 2, SUB, D], F32)
        sum_t = sb("sum_t", [P, HALVES, ROWS], F32)
        h_t = sb("h_t", [P, HALVES, ROWS], F32)
        w1 = sb("w1", [P, HALVES, D], F32)
        w2 = sb("w2", [P, HALVES, D], F32)
        c_row = sb("c_row", [P, D], F32)
        ident16 = sb("ident16", [P, P], F16)
        fold = sb("fold", [P, QUAD, P], F16)
        layer = sb("layer", [P, 2, D], F32)
        deg_part = sb("deg_part", [P, 2, GROUPS], F32)
        deg16 = sb("deg16", [P, GROUPS], F16)
        deg = sb("deg", [P, SUB], F32)
        rdeg = sb("rdeg", [P, SUB], F32)

        spare = mask_t[:, 1, :, :, :].rearrange("p c g l -> p (c g l)").bitcast(F32)
        cursor = [0]

        def early(n):
            cursor[0] += n
            assert cursor[0] <= CHUNKS * ROWS
            return spare[:, cursor[0] - n:cursor[0]]

        x_ring = [early(SUB * D).rearrange("p (s d) -> p s d", s=SUB) for _ in range(XRING - 4)]
        x_ring += [x_again[:, n, :, :] for n in range(2)]
        x_ring += [t[:, :, :].rearrange("p h r -> p (h r)").rearrange("p (s d) -> p s d", s=SUB) for t in (sum_t, h_t)]
        ws = early(HALVES * D).rearrange("p (h n) -> p h n", h=HALVES)
        wn = early(HALVES * D).rearrange("p (h n) -> p h n", h=HALVES)
        wc = early(2 * HALVES * D).rearrange("p (h n) -> p h n", h=2 * HALVES)
        ws_t = early(HALVES * D).rearrange("p (m k) -> p m k", m=HALVES)
        wn_t = early(HALVES * D).rearrange("p (m k) -> p m k", m=HALVES)
        ident = early(P)
        ones = early(P)
        b_cols = early(2 * HALVES)
        b_wide = early(2 * HALVES * P).rearrange("p (h m) -> p h m", h=2 * HALVES)
        bc_row = layer[:, 0, :]
        few = sb("few", [P, 512], F32)
        taken = [0]

        def small(n):
            taken[0] += n
            return few[:, taken[0] - n:taken[0]]

        stats = small(2 * SUB * 6).rearrange("p (e s k) -> p e s k", e=2, s=SUB)
        mean_var = small(CHUNKS * SUB * 2).rearrange("p (e s k) -> p e s k", e=CHUNKS, s=SUB)
        var_s = small(2 * SUB).rearrange("p (e s) -> p e s", e=2)
        rstd = small(CHUNKS * SUB).rearrange("p (e s) -> p e s", e=CHUNKS)
        shift = small(CHUNKS * SUB).rearrange("p (e s) -> p e s", e=CHUNKS)
        power = small(2 * SUB).rearrange("p (e s) -> p e s", e=2)

        banks = [ctx.enter_context(nc.psum_tensor(f"bank{n}", [P, ROWS], F32)) for n in range(8)]
        sum_ps = [banks[0:2], banks[2:4]]
        h_ps = banks[4:6]
        out_ps = [b[:, :].rearrange("p (w n) -> p w n", w=2) for b in banks[6:8]]
        last_ps = out_ps + [b[:, :].rearrange("p (w n) -> p w n", w=2) for b in h_ps]
        self_c = mask_t[:, 0, 0:SUB * D // ROWS, :, :].rearrange("p c g l -> p (c g l)").bitcast(F32)

        stage_full = [sem(f"stage_full{n}") for n in range(STAGES)]
        masked = sem("masked")
        transposed = sem("transposed")
        counted_rows = sem("counted_rows")
        x_full = [sem(f"x_full{n}") for n in range(XRING)]
        stats_done = sem("stats_done")
        aggr_done = sem("aggr_done")
        var_ready = sem("var_ready")
        rstd_ready = sem("rstd_ready")
        normed = sem("normed")
        clipped = sem("clipped")
        high_ready = sem("high_ready")
        shift_ready = sem("shift_ready")
        low_pool = sem("low_pool")
        low_dve = sem("low_dve")
        w_loaded = sem("w_loaded")
        zeroed = sem("zeroed")
        ident_ready = sem("ident_ready")
        fold_ready = sem("fold_ready")
        wide_ready = sem("wide_ready")
        w_turned = sem("w_turned")
        wt_ready = sem("wt_ready")
        w_product = sem("w_product")
        w_ready = sem("w_ready")
        main_done = sem("main_done")
        sum_copied = sem("sum_copied")
        sum_copied_dve = sem("sum_copied_dve")
        self_last = sem("self_last")
        self_ready = sem("self_ready")
        h_turned = sem("h_turned")
        h_copied = sem("h_copied")
        deg16_ready = sem("deg16_ready")
        deg_summed = sem("deg_summed")
        deg_clamped = sem("deg_clamped")
        rdeg_ready = sem("rdeg_ready")
        projected = sem("projected")
        out_read = sem("out_read")
        added = sem("added")
        x_again_full = [sem(f"x_again_full{n}") for n in range(2)]
        out_ready = sem("out_ready")
        stored = sem("stored")

        block = ctx.enter_context(nc.Block())

        def mask_words(n_slot):
            return mask[:, n_slot, :].bitcast(U32)

        def wait_lows(eng, e):
            by_vector = up_to(e, LOW_ON_VECTOR)
            by_pool = e + 1 - by_vector
            eng.wait_ge(low_pool, by_pool)
            if by_vector:
                eng.wait_ge(low_dve, by_vector)

        @block.sync
        def _(sp):
            def load_group(s, g):
                sub, a = divmod(g, QUAD)
                for q in range(QUAD):
                    sp.dma_start(stage[LANE * q:LANE * (q + 1), g % STAGES, :],
                                 adj_v[a, s, :, sub, q, :]).then_inc(stage_full[g % STAGES], DONE)

            def load_x(dst, s, q, signal):
                sp.dma_start(dst[LANE * q:LANE * (q + 1), :], x_v[q, s, :, :]).then_inc(signal, DONE)

            for e in range(CHUNKS):
                if e >= XRING:
                    wait_lows(sp, e - XRING)
                for q in range(QUAD):
                    load_x(x_ring[e % XRING].rearrange("p s d -> p (s d)"), e, q, x_full[e % XRING])
                if e == 3:
                    for dst, w in ((wc, w_comb), (ws, w_self), (wn, w_nb)):
                        sp.dma_start(dst, w.rearrange("(h p) n -> p h n", p=P)).then_inc(w_loaded, DONE)
                    sp.dma_start(bc_row, b_comb.rearrange("(a n) -> a n", a=1).partition_broadcast(P)
                                 ).then_inc(w_loaded, DONE)
                    for n, b in enumerate((b_self, b_nb)):
                        sp.dma_start(b_cols[:, n * HALVES:(n + 1) * HALVES], b.rearrange("(h p) -> p h", p=P),
                                     allow_slow_non_contiguous=True).then_inc(w_loaded, DONE)
                for g in GROUPS_OF_PAIR[e // 2] if e % 2 else []:
                    if g >= STAGES:
                        sp.wait_ge(masked, g - STAGES + 1)
                    load_group(0, g)

            def load_chunk(s, g0, g1):
                for g in range(g0, g1):
                    sp.wait_ge(masked, s * GROUPS + (g - STAGES + 1))
                    load_group(s, g)

            def reload_x(s, parity, first=False):
                if not first:
                    sp.wait_ge(stored, (s - 1) * (QUAD * DONE))
                for q in range(QUAD):
                    load_x(x_again[:, parity, :, :].rearrange("p s d -> p (s d)"), s, q, x_again_full[parity])

            def store(s, parity, sub0=0, subs=SUB):
                sp.wait_ge(out_ready, s * SUB + (sub0 + subs))
                for q in range(QUAD):
                    sp.dma_start(out_v[q, s, :, sub0 * D:(sub0 + subs) * D],
                                 x_again[LANE * q:LANE * (q + 1), parity, sub0:sub0 + subs, :]
                                 .rearrange("p s d -> p (s d)")).then_inc(stored, DONE)

            load_chunk(0, FIRST_GROUPS, GROUPS)
            load_chunk(1, 0, 4)
            wait_lows(sp, CHUNKS - 1)
            reload_x(0, 0, first=True)
            load_chunk(1, 4, 8)
            reload_x(1, 1, first=True)
            load_chunk(1, 8, GROUPS)
            with sp.Fori(0, PAIRS) as k:
                for par in range(2):
                    s = k * 2 + (2 + par)
                    load_chunk(s, 0, GROUPS)
                    store(k * 2 + par, par)
                    reload_x(k * 2 + (2 + par), par)
            store(CHUNKS - 2, 0)
            store(CHUNKS - 1, 1, 0, SUB // 2)
            store(CHUNKS - 1, 1, SUB // 2, SUB // 2)
            sp.wait_ge(stored, (CHUNKS + 1) * QUAD * DONE)

        @block.gpsimd
        def _(pool):
            pool.memset(ident, 0.0).then_inc(zeroed, 1)
            pool.memset(ones, 1.0).then_inc(zeroed, 1)
            pool.memset(power, -0.5).then_inc(zeroed, 1)
            pool.memset(fold[:, :, :], 0.0).then_inc(zeroed, 1)
            pool.wait_ge(zeroed, 4)
            pool.affine_select(out=ident, in_=ident, compare_op=ALU.not_equal, fill=1.0, base=0,
                               pattern=[[-1, P]], channel_multiplier=1).then_inc(ident_ready, 1)

            def rstd_of(pair):
                two = slice(2 * pair, 2 * pair + 2)
                pool.wait_ge(aggr_done, 2 * SUB * (pair + 1))
                pool.tensor_scalar(var_s, mean_var[:, two, :, 1], EPS, SCALE ** -2,
                                   ALU.add, ALU.mult).then_inc(var_ready, 1)
                pool.wait_ge(var_ready, pair + 1)
                pool.tensor_tensor(rstd[:, two, :], var_s, power, ALU.pow).then_inc(rstd_ready, 1)

            def remainder(e):
                pool.wait_ge(high_ready, e + 1)
                tiles = slice(SUB * e, SUB * (e + 1))
                pool.tensor_tensor(h16[:, 1, tiles, :], x_ring[e % XRING], h16[:, 0, tiles, :],
                                   ALU.subtract).then_inc(low_pool, 1)

            for pair in range(CHUNKS // 2 + 2):
                for e in (2 * pair - 4, 2 * pair - 3):
                    if e % 2 and 2 * pair < CHUNKS:
                        rstd_of(pair)
                    if e >= 0 and e not in LOW_ON_VECTOR:
                        remainder(e)

        @block.scalar
        def _(act):
            def count(s, g, parity):
                act.wait_ge(masked, s * GROUPS + (g + 1))
                if not (isinstance(s, int) and s == 0 and g < 2):
                    act.wait_ge(counted_rows, s * GROUPS + (g - 1))
                act.activation(counted[:, g % 2, :], mask[:, g % MASKS, :], ACT.Copy,
                               accum_out=deg_part[:, parity, g:g + 1]).then_inc(counted_rows, 1)

            for e in range(CHUNKS):
                t = x_ring[e % XRING]
                if e in COUNTS_BEFORE:
                    count(0, COUNTS_BEFORE[e], 0)
                if e in NORM_ON_VECTOR:
                    act.wait_ge(normed, up_to(e, NORM_ON_VECTOR) * SUB)
                else:
                    act.wait_ge(shift_ready, e // 2 + 1)
                    for sub in range(SUB):
                        act.activation(t[:, sub, :], t[:, sub, :], ACT.Relu, bias=shift[:, e, sub:sub + 1],
                                       scale=rstd[:, e, sub:sub + 1]).then_inc(clipped, 1)
                    act.wait_ge(clipped, (e + 1 - up_to(e, NORM_ON_VECTOR)) * SUB)
                act.activation(h16[:, 0, SUB * e:SUB * (e + 1), :], t, ACT.Relu).then_inc(high_ready, 1)
                if e == 0:
                    act.wait_ge(w_loaded, 6 * DONE)
                    act.wait_ge(zeroed, 4)
                    for j in range(2 * HALVES):
                        act.activation(b_wide[:, j, :], ones, ACT.Copy, scale=b_cols[:, j:j + 1]).then_inc(wide_ready, 1)
                if e == 1:
                    act.wait_ge(w_turned, 1)
                    act.activation(ws_t.rearrange("p m k -> p (m k)"), banks[4][:, :], ACT.Copy).then_inc(wt_ready, 1)
                    act.activation(wn_t.rearrange("p m k -> p (m k)"), banks[5][:, :], ACT.Copy).then_inc(wt_ready, 1)
            act.wait_ge(w_product, 1)
            act.activation(w1[:, :, :].rearrange("p h n -> p (h n)"), banks[6][:, :], ACT.Copy).then_inc(w_ready, 1)
            act.activation(w2[:, :, :].rearrange("p h n -> p (h n)"), banks[7][:, :], ACT.Copy).then_inc(w_ready, 1)
            for g in range(len(COUNTS_BEFORE), GROUPS):
                count(0, g, 0)

            def chunk_counts(s, parity, g0=0, g1=GROUPS, wait=False):
                if wait:
                    act.wait_ge(deg16_ready, s - 1)
                for g in range(g0, g1):
                    count(s, g, parity)

            def drain_h(s):
                act.wait_ge(h_turned, s + 1)
                for half in range(HALVES):
                    act.activation(h_t[:, half, :], h_ps[half][:, :], ACT.Copy).then_inc(h_copied, 1)

            def drain_sum(s, parity, halves=range(HALVES)):
                act.wait_ge(main_done, s + 1)
                for half in halves:
                    act.activation(sum_t[:, half, :], sum_ps[parity][half][:, :], ACT.Copy).then_inc(sum_copied, 1)

            def drain(s, parity, first=False):
                if first:
                    wait_lows(act, CHUNKS - 1)
                else:
                    act.wait_ge(projected, s * SUB)
                drain_sum(s, parity)
                drain_h(s)

            chunk_counts(1, 1, 0, 4)
            drain(0, 0, first=True)
            chunk_counts(1, 1, 4)
            chunk_counts(2, 0, 0, 9, wait=True)
            drain(1, 1)
            chunk_counts(2, 0, 9)
            chunk_counts(3, 1, wait=True)
            with act.Fori(1, PAIRS) as k:
                for par in range(2):
                    drain(k * 2 + par, par)
                    chunk_counts(k * 2 + (2 + par), par, wait=True)
            drain(CHUNKS - 2, 0)
            act.wait_ge(projected, (CHUNKS - 1) * SUB)
            drain_h(CHUNKS - 1)
            drain_sum(CHUNKS - 1, 1, [0])

        @block.tensor
        def _(pe):
            pe.wait_ge(w_loaded, 6 * DONE)
            pe.wait_ge(ident_ready, 2)
            for w, bank in ((ws, banks[4]), (wn, banks[5])):
                for m in range(HALVES):
                    for kk in range(HALVES):
                        at = m * D + kk * P
                        mm = pe.transpose(bank[:, at:at + P], w[:, kk, m * P:(m + 1) * P], ident)
            mm.then_inc(w_turned, 1)
            pe.wait_ge(wt_ready, 2)
            for n, (w_t, bank) in enumerate(((ws_t, banks[6]), (wn_t, banks[7]))):
                for kk in range(HALVES):
                    for m in range(HALVES):
                        pe.matmul(bank[:, kk * D:(kk + 1) * D], w_t[:, m, kk * P:(kk + 1) * P],
                                  wc[:, n * HALVES + m, :], start=(m == 0), stop=(m == HALVES - 1))
            pe.wait_ge(wide_ready, 2 * HALVES)
            for m in range(2 * HALVES):
                mm = pe.matmul(banks[3][:, 0:D], b_wide[:, m, :], wc[:, m, :],
                               start=(m == 0), stop=(m == 2 * HALVES - 1))
            mm.then_inc(w_product, 1)

            def sum_step(parity, e, sub, rows=slice(0, ROWS)):
                words = mask_t[:, parity, e, :, :].rearrange("p g l -> p (g l)").bitcast(FP8)
                rhs = words.rearrange("p (i s) -> p i s", s=SUB)[:, rows, sub]
                for half in range(HALVES):
                    for part in range(2):
                        mm = pe.matmul(sum_ps[parity][half][:, rows],
                                       h16[:, part, SUB * e + sub, half * P:(half + 1) * P], rhs,
                                       start=(rows.start == 0 and e == 0 and sub == 0 and part == 0),
                                       stop=(rows.stop == ROWS and e == CHUNKS - 1 and sub == SUB - 1 and part == 1))
                return mm

            def turn_h(s, first=False):
                if not first:
                    pe.wait_ge(h_copied, s * HALVES)
                for half in range(HALVES):
                    for sub in range(SUB):
                        for part in range(2):
                            lhs = h16[:, part, bass.ds(s * SUB + sub, 1), half * P:(half + 1) * P]
                            mm = pe.matmul(h_ps[half][:, sub * P:(sub + 1) * P],
                                           lhs.rearrange("p o d -> p (o d)"), ident16[:, :],
                                           start=(part == 0), stop=(part == 1))
                mm.then_inc(h_turned, 1)

            def sum_degrees(s, bank, first=False):
                if first:
                    pe.wait_ge(fold_ready, QUAD * QUAD)
                pe.wait_ge(deg16_ready, s + 1)
                for a in range(QUAD):
                    mm = pe.matmul(bank[:, 0:SUB], fold[:, a, :], deg16[:, a:GROUPS:QUAD],
                                   start=(a == 0), stop=(a == QUAD - 1))
                mm.then_inc(deg_summed, 1)

            def project(s, sub, first=False):
                if sub == 0:
                    pe.wait_ge(h_copied, s * HALVES + HALVES)
                if not (first and sub < 2):
                    pe.wait_ge(out_read, s * SUB + (sub - 1))
                rows = slice(sub * P, (sub + 1) * P)
                for n, (src, w) in enumerate(((h_t, w1), (sum_t, w2))):
                    for half in range(HALVES):
                        mm = pe.matmul(out_ps[sub % 2][:, n, :], src[:, half, rows], w[:, half, :],
                                       start=(half == 0), stop=(half == HALVES - 1))
                mm.then_inc(projected, 1)

            def chunk(s, parity, before, parts=1, projections=(11, 19, 27, 35), first=False):
                if first:
                    pe.wait_ge(w_ready, 3)
                else:
                    pe.wait_ge(rdeg_ready, s - 1)
                if parts == 1:
                    pe.wait_ge(transposed, s * GROUPS + GROUPS)
                turn_h(before, first)
                for part in range(parts):
                    if parts > 1:
                        pe.wait_ge(transposed, s * GROUPS + (part + 1) * (GROUPS // parts))
                    rows = slice(part * (ROWS // parts), (part + 1) * (ROWS // parts))
                    for tile in range(TILES):
                        mm = sum_step(parity, tile // SUB, tile % SUB, rows)
                        at, rest = divmod(part * TILES + tile, parts)
                        if rest:
                            continue
                        if at == 7:
                            pe.wait_ge(sum_copied, before * HALVES + HALVES)
                            sum_degrees(before, sum_ps[1 - parity][0], first)
                        if at in projections:
                            project(before, projections.index(at), first)
                        if s is last:
                            ahead_of_last(at)
                mm.then_inc(main_done, 1)

            last = CHUNKS - 1

            def project_last(sub, n, src, w):
                for half in range(HALVES):
                    mm = pe.matmul(last_ps[sub][:, n, :], src[:, half, sub * P:(sub + 1) * P], w[:, half, :],
                                   start=(half == 0), stop=(half == HALVES - 1))
                return mm

            def ahead_of_last(at):
                if at == 40:
                    turn_h(last)
                if at == 48:
                    sum_degrees(last, sum_ps[(last - 1) % 2][0])
                if at == 52:
                    pe.wait_ge(h_copied, (last + 1) * HALVES)
                    pe.wait_ge(out_read, last * SUB)
                    for sub in range(SUB):
                        mm = project_last(sub, 0, h_t, w1)
                    mm.then_inc(self_last, 1)

            QUARTER = GROUPS // 4
            SECOND_QUARTER = (9, lambda e: 0 if e < 9 else min(e + 1, 4 * e - 34))

            def quarter(n, e):
                for sub in range(SUB):
                    mm = sum_step(0, e, sub, slice(n * P, (n + 1) * P))
                return mm

            pe.wait_ge(transposed, QUARTER)
            behind = 0
            for e in range(CHUNKS):
                wait_lows(pe, e)
                quarter(0, e)
                if e == SECOND_QUARTER[0]:
                    pe.wait_ge(transposed, 2 * QUARTER)
                while behind < SECOND_QUARTER[1](e):
                    quarter(1, behind)
                    behind += 1
            for n in range(2, 4):
                pe.wait_ge(transposed, (n + 1) * QUARTER)
                for e in range(CHUNKS):
                    mm = quarter(n, e)
            mm.then_inc(main_done, 1)

            chunk(1, 1, 0, parts=4, first=True)
            chunk(2, 0, 1, parts=2, projections=(9, 11, 13, 15))
            with pe.Fori(1, PAIRS) as k:
                for par in (1, 0):
                    chunk(k * 2 + (2 - par), par, k * 2 + (1 - par))
            chunk(last, last % 2, last - 1)
            pe.wait_ge(sum_copied, (last + 1) * HALVES - 1)
            pe.wait_ge(sum_copied_dve, 1)
            for sub in range(SUB):
                project_last(sub, 1, sum_t, w2).then_inc(projected, 1)

        @block.vector
        def _(dve):
            def form_mask(s, g):
                dve.wait_ge(stage_full[g % STAGES],
                            (s * (GROUPS // STAGES) + (g // STAGES + 1)) * (QUAD * DONE))
                if not (isinstance(s, int) and s == 0 and g < MASKS):
                    dve.wait_ge(counted_rows, s * GROUPS + (g - MASKS + 1))
                    dve.wait_ge(transposed, s * GROUPS + (g - MASKS + 1))
                dve.tensor_scalar(mask[:, g % MASKS, :], stage[:, g % STAGES, :], 0.0, float(ONE_BYTE),
                                  ALU.is_gt, ALU.mult).then_inc(masked, 1)

            def turn_mask(s, g, parity):
                dve.wait_ge(masked, s * GROUPS + (g + 1))
                src = mask_words(g % MASKS).rearrange("p (c l) -> p c l", l=LANE)
                dve.transpose(mask_t[:, parity, :, g, :], src).then_inc(transposed, 1)

            def stats_of(e):
                dve.wait_ge(x_full[e % XRING], (e // XRING + 1) * QUAD * DONE)
                for sub in range(SUB):
                    dve.bn_stats(stats[:, e % 2, sub, :], x_ring[e % XRING][:, sub, :]).then_inc(stats_done, 1)
                dve.wait_ge(stats_done, (e + 1) * SUB)
                for sub in range(SUB):
                    dve.bn_aggr(mean_var[:, e, sub, :], stats[:, e % 2, sub, :]).then_inc(aggr_done, 1)

            def normalise(pair):
                dve.wait_ge(rstd_ready, pair + 1)
                dve.scalar_tensor_tensor(shift[:, 2 * pair:2 * pair + 2, :], mean_var[:, 2 * pair:2 * pair + 2, :, 0], -1.0,
                                         rstd[:, 2 * pair:2 * pair + 2, :], ALU.mult, ALU.mult).then_inc(shift_ready, 1)
                for e in (2 * pair, 2 * pair + 1):
                    for sub in range(SUB if e in NORM_ON_VECTOR else 0):
                        t = x_ring[e % XRING][:, sub, :]
                        dve.tensor_scalar(t, t, mean_var[:, e, sub, 0:1], rstd[:, e, sub:sub + 1],
                                          ALU.subtract, ALU.mult).then_inc(normed, 1)

            def remainder(e):
                dve.wait_ge(high_ready, e + 1)
                tiles = slice(SUB * e, SUB * (e + 1))
                flat = "p s d -> p (s d)"
                dve.scalar_tensor_tensor(h16[:, 1, tiles, :].rearrange(flat), x_ring[e % XRING].rearrange(flat), 0.0,
                                         h16[:, 0, tiles, :].rearrange(flat), ALU.max, ALU.subtract
                                         ).then_inc(low_dve, 1)

            def pack(s, parity, first=False):
                dve.wait_ge(counted_rows, s * GROUPS + GROUPS)
                if not first:
                    dve.wait_ge(deg_summed, s)
                dve.tensor_scalar(deg16[:, :], deg_part[:, parity, :], 1.0 / ONE_BYTE, None, ALU.mult).then_inc(deg16_ready, 1)

            def invert_degrees(s, bank):
                dve.wait_ge(deg_summed, s + 1)
                dve.tensor_scalar(deg[:, :], bank[:, 0:SUB], 1.0, EDGE * SCALE, ALU.max, ALU.mult
                                  ).then_inc(deg_clamped, 1)
                dve.wait_ge(deg_clamped, s + 1)
                dve.reciprocal(rdeg[:, :], deg[:, :]).then_inc(rdeg_ready, 1)

            def finish(pair, parity, sub):
                s = pair * 2 + parity
                dve.wait_ge(projected, s * SUB + (sub + 1))
                if sub == 0:
                    dve.wait_ge(rdeg_ready, s + 1)
                    dve.wait_ge(x_again_full[parity], (pair + 1) * (QUAD * DONE))
                y = layer[:, sub % 2, :]
                xa = x_again[:, parity, sub, :]
                dve.scalar_tensor_tensor(y, out_ps[sub % 2][:, 1, :], rdeg[:, sub:sub + 1], c_row[:, :],
                                         ALU.mult, ALU.add).then_inc(added, 1)
                dve.wait_ge(added, s * SUB + (sub + 1))
                dve.scalar_tensor_tensor(y, out_ps[sub % 2][:, 0, :], 1.0 / SCALE, y,
                                         ALU.mult, ALU.add).then_inc(out_read, 1)
                dve.wait_ge(out_read, s * SUB + (sub + 1))
                dve.scalar_tensor_tensor(xa, y, 0.0, xa, ALU.max, ALU.add).then_inc(out_ready, 1)

            dve.wait_ge(ident_ready, 1)
            dve.tensor_copy(ident16[:, :], ident).then_inc(ident_ready, 1)
            for q in range(QUAD):
                rows = slice(LANE * q, LANE * (q + 1))
                for a in range(QUAD):
                    dve.tensor_copy(fold[rows, a, LANE * a:LANE * (a + 1)], ident[rows, rows]
                                    ).then_inc(fold_ready, 1)

            for pair in range(CHUNKS // 2 + 2):
                groups = GROUPS_OF_PAIR[pair] if 2 * pair < CHUNKS else []
                if 2 * pair < CHUNKS:
                    stats_of(2 * pair)
                if 1 <= pair <= CHUNKS // 2:
                    normalise(pair - 1)
                if 2 * pair < CHUNKS:
                    stats_of(2 * pair + 1)
                for g in groups:
                    form_mask(0, g)
                for g in groups:
                    turn_mask(0, g, 0)
                for e in (2 * pair - 4, 2 * pair - 3):
                    if e >= 0 and e in LOW_ON_VECTOR:
                        remainder(e)
            for g in range(FIRST_GROUPS, GROUPS):
                form_mask(0, g)
                turn_mask(0, g, 0)

            dve.wait_ge(w_product, 1)
            dve.tensor_tensor(c_row[:, :], banks[3][:, 0:D], bc_row, ALU.add).then_inc(w_ready, 1)

            for g in range(GROUPS):
                form_mask(1, g)
                if g == 0:
                    wait_lows(dve, CHUNKS - 1)
                    dve.wait_ge(w_ready, 3)
                else:
                    turn_mask(1, g - 1, 1)
                if g == 5:
                    pack(0, 0, first=True)
                if g == 6:
                    invert_degrees(0, sum_ps[0][0])
                if g in (8, 10, 12, 14):
                    finish(0, 0, (g - 8) // 2)
            turn_mask(1, GROUPS - 1, 1)

            for g in range(GROUPS):
                form_mask(2, g)
                if g == 0:
                    dve.wait_ge(main_done, 1)
                else:
                    turn_mask(2, g - 1, 0)
                if g == 7:
                    pack(1, 1)
                if g == 11:
                    invert_degrees(1, sum_ps[1][0])
                if g >= 12:
                    finish(0, 1, g - 12)
            turn_mask(2, GROUPS - 1, 0)

            for g in range(GROUPS):
                form_mask(3, g)
                if g == 0:
                    dve.wait_ge(main_done, 2)
                else:
                    turn_mask(3, g - 1, 1)
                if g == 3:
                    pack(2, 0)
            turn_mask(3, GROUPS - 1, 1)

            with dve.Fori(2, PAIRS + 1) as k:
                for par in range(2):
                    s = k * 2 + par
                    for g in range(GROUPS):
                        form_mask(s, g)
                        if g == 0:
                            dve.wait_ge(main_done, s - 1)
                        else:
                            turn_mask(s, g - 1, par)
                        if g == 3:
                            invert_degrees(s - 2, sum_ps[par][0])
                            pack(s - 1, 1 - par)
                        if g in (5, 7, 9, 11):
                            finish(k - 1, par, (g - 5) // 2)
                    turn_mask(s, GROUPS - 1, par)
            last = CHUNKS - 1
            invert_degrees(last - 1, sum_ps[0][0])
            pack(last, 1)
            for sub in range(SUB):
                finish(last // 2, 0, sub)

            invert_degrees(last, sum_ps[0][0])
            dve.wait_ge(self_last, 1)
            dve.wait_ge(main_done, last)
            for sub in range(SUB):
                dve.scalar_tensor_tensor(self_c[:, sub * D:(sub + 1) * D], last_ps[sub][:, 0, :], 1.0 / SCALE,
                                         c_row[:, :], ALU.mult, ALU.add).then_inc(self_ready, 1)
            dve.wait_ge(rdeg_ready, last + 1)
            dve.wait_ge(x_again_full[1], (last // 2 + 1) * (QUAD * DONE))
            dve.wait_ge(self_ready, SUB)
            dve.wait_ge(main_done, last + 1)
            dve.tensor_copy(sum_t[:, 1, :], sum_ps[1][1][:, :]).then_inc(sum_copied_dve, 1)
            for sub in range(SUB):
                dve.wait_ge(projected, last * SUB + (sub + 1))
                y = layer[:, sub % 2, :]
                xa = x_again[:, 1, sub, :]
                dve.scalar_tensor_tensor(y, last_ps[sub][:, 1, :], rdeg[:, sub:sub + 1],
                                         self_c[:, sub * D:(sub + 1) * D], ALU.mult, ALU.add).then_inc(added, 1)
                dve.wait_ge(added, last * SUB + (sub + 1))
                dve.scalar_tensor_tensor(xa, y, 0.0, xa, ALU.max, ALU.add).then_inc(out_ready, 1)


_INS = ["x", "adj", "L0_gnn_W_self", "L0_gnn_b_self", "L0_gnn_W_nb", "L0_gnn_b_nb", "L0_gnn_W_comb", "L0_gnn_b_comb"]


def kernel(**inputs):
    import numpy as np
    import concourse.bacc as bacc
    from concourse.bass_utils import run_bass_kernel_spmd

    nc = bacc.Bacc("TRN2", target_bir_lowering=False, num_devices=1)
    arrays, args = {}, []
    for name in _INS:
        a = np.ascontiguousarray(inputs[name])
        arrays[f"in_{name}_dram"] = a
        args.append(nc.dram_tensor(f"in_{name}_dram", a.shape, mybir.dt.from_np(a.dtype), kind="ExternalInput").ap())
    shape = arrays["in_x_dram"].shape
    out = nc.dram_tensor("out_0_dram", shape, F32, kind="ExternalOutput").ap()
    graph_layer(nc, *args, out)
    r = run_bass_kernel_spmd(nc, [arrays], core_ids=[0])
    return r.results[0]["out_0_dram"]
```

```python
from contextlib import ExitStack

import concourse.bass as bass
from concourse import mybir

F32 = mybir.dt.float32
F16 = mybir.dt.float16
FP8 = mybir.dt.float8e4
I32 = mybir.dt.int32
U32 = mybir.dt.uint32
U8 = mybir.dt.uint8
ALU = mybir.AluOpType
ACT = mybir.ActivationFunctionType

P = 128
QUAD = 4
LANE = P // QUAD
SUB = 4
SCALE = 2.0 ** 11
ONE_BYTE = 32
EDGE = 2.0 ** -3
W_SCALE = 2.0 ** 8
HIGH_SCALE = 2.0 ** -10
SELF_SCALE = SCALE * W_SCALE
NB_SCALE = SCALE * EDGE * HIGH_SCALE * W_SCALE
EPS = 1e-5

STAGES = 4
MASKS = 8
XRING = 8
DONE = 16

GROUPS_OF_PAIR = [[0], [1], [2, 3], [4], [5], [6, 7], [], []]
FIRST_GROUPS = sum(map(len, GROUPS_OF_PAIR))
MASKS_OF_PAIR = GROUPS_OF_PAIR + [[8], [9]]


NORM_ON_VECTOR = (5, 11, 14, 15)
LOW_ON_VECTOR = (5, 9, 11, 14, 15)
COUNTS_BEFORE = {4: 0, 6: 1, 12: 2}


def up_to(e, some):
    return sum(i <= e for i in some)


def graph_layer(nc, x, adj, w_self, b_self, w_nb, b_nb, w_comb, b_comb, out):
    N, D = x.shape
    HALVES = D // P
    SPAN = N // QUAD
    WORDS = SPAN // SUB
    CHUNKS = SPAN // (LANE * SUB)
    ROWS = N // CHUNKS
    GROUPS = ROWS // LANE
    TILES = N // P
    PAIRS = (CHUNKS - 2) // 2
    assert D == 2 * P and ROWS == 512 and GROUPS == 16 and CHUNKS % 2 == 0
    assert GROUPS % STAGES == 0 and GROUPS % MASKS == 0 and CHUNKS % XRING == 0

    adj_v = adj.rearrange("(a c l s) (b f) -> a c l s b f", a=QUAD, c=CHUNKS, l=LANE, s=SUB, b=QUAD)
    x_v = x.rearrange("(a c l s) d -> a c l (s d)", a=QUAD, c=CHUNKS, l=LANE, s=SUB)
    out_v = out.rearrange("(a c l s) d -> a c l (s d)", a=QUAD, c=CHUNKS, l=LANE, s=SUB)

    with ExitStack() as ctx:
        def sb(name, shape, dt):
            return ctx.enter_context(nc.sbuf_tensor(name, shape, dt))

        def sem(name):
            return ctx.enter_context(nc.semaphore(name))

        mask_t = sb("mask_t", [P, 2, CHUNKS, GROUPS, LANE], U32)
        h16 = sb("h16", [P, 2, TILES, D], F16)
        stage = sb("stage", [P, STAGES, SPAN], I32)
        mask = sb("mask", [P, MASKS, SPAN], U8)
        counted = sb("counted", [P, 2, SPAN], U8)
        x_again = sb("x_again", [P, 2, SUB, D], F32)
        sum_t = sb("sum_t", [P, HALVES, 2, ROWS], F16)
        h_t = sb("h_t", [P, HALVES, 2, ROWS], F16)
        w1 = sb("w1", [P, 2, HALVES, D], F16)
        w2 = sb("w2", [P, 3, HALVES, D], F16)
        c_row = sb("c_row", [P, D], F32)
        ident16 = sb("ident16", [P, P], F16)
        fold = sb("fold", [P, QUAD, P], F16)
        layer = sb("layer", [P, 2, D], F32)
        deg_part = sb("deg_part", [P, 2, GROUPS], F32)
        deg16 = sb("deg16", [P, GROUPS], F16)
        deg = sb("deg", [P, SUB], F32)
        rdeg = sb("rdeg", [P, SUB], F32)

        spare = mask_t[:, 1, :, :, :].rearrange("p c g l -> p (c g l)").bitcast(F32)
        cursor = [0]

        def early(n):
            cursor[0] += n
            assert cursor[0] <= CHUNKS * ROWS
            return spare[:, cursor[0] - n:cursor[0]]

        x_ring = [early(SUB * D).rearrange("p (s d) -> p s d", s=SUB) for _ in range(XRING - 4)]
        x_ring += [x_again[:, n, :, :] for n in range(2)]
        x_ring += [t[:, :, :, :].rearrange("p h w r -> p (h w r)").bitcast(F32).rearrange("p (s d) -> p s d", s=SUB)
                   for t in (sum_t, h_t)]
        ws = early(HALVES * D).rearrange("p (h n) -> p h n", h=HALVES)
        wn = early(HALVES * D).rearrange("p (h n) -> p h n", h=HALVES)
        wc = early(2 * HALVES * D).rearrange("p (h n) -> p h n", h=2 * HALVES)
        ws_t = early(HALVES * D).rearrange("p (m k) -> p m k", m=HALVES)
        wn_t = early(HALVES * D).rearrange("p (m k) -> p m k", m=HALVES)
        ident = early(P)
        ones = early(P)
        b_cols = early(2 * HALVES)
        b_wide = early(2 * HALVES * P).rearrange("p (h m) -> p h m", h=2 * HALVES)
        bc_row = layer[:, 0, :]
        few = sb("few", [P, 320], F32)
        taken = [0]

        def small(n):
            taken[0] += n
            return few[:, taken[0] - n:taken[0]]

        stats = small(2 * SUB * 6).rearrange("p (e s k) -> p e s k", e=2, s=SUB)
        mean_var = small(CHUNKS * SUB * 2).rearrange("p (e s k) -> p e s k", e=CHUNKS, s=SUB)
        var_s = small(2 * SUB).rearrange("p (e s) -> p e s", e=2)
        rstd = small(CHUNKS * SUB).rearrange("p (e s) -> p e s", e=CHUNKS)
        shift = small(CHUNKS * SUB).rearrange("p (e s) -> p e s", e=CHUNKS)
        power = small(2 * SUB).rearrange("p (e s) -> p e s", e=2)

        banks = [ctx.enter_context(nc.psum_tensor(f"bank{n}", [P, ROWS], F32)) for n in range(8)]
        sum_ps = [banks[0:2], banks[2:4]]
        h_ps = [b[:, :].bitcast(F16).rearrange("p (w r) -> p w r", w=2) for b in banks[4:6]]
        out_ps = [b[:, :].rearrange("p (w n) -> p w n", w=2) for b in banks[6:8]]
        last_ps = out_ps + [b[:, :].rearrange("p (w n) -> p w n", w=2) for b in banks[4:6]]
        self_c = mask_t[:, 0, 0:SUB * D // ROWS, :, :].rearrange("p c g l -> p (c g l)").bitcast(F32)

        stage_full = [sem(f"stage_full{n}") for n in range(STAGES)]
        masked = sem("masked")
        transposed = sem("transposed")
        counted_rows = sem("counted_rows")
        x_full = [sem(f"x_full{n}") for n in range(XRING)]
        stats_done = sem("stats_done")
        aggr_done = sem("aggr_done")
        var_ready = sem("var_ready")
        rstd_ready = sem("rstd_ready")
        normed = sem("normed")
        clipped = sem("clipped")
        high_ready = sem("high_ready")
        shift_ready = sem("shift_ready")
        low_pool = sem("low_pool")
        low_dve = sem("low_dve")
        w_loaded = sem("w_loaded")
        zeroed = sem("zeroed")
        ident_ready = sem("ident_ready")
        fold_ready = sem("fold_ready")
        wide_ready = sem("wide_ready")
        w_turned = sem("w_turned")
        wt_ready = sem("wt_ready")
        w_product = sem("w_product")
        w_high = sem("w_high")
        w_ready = sem("w_ready")
        main_done = sem("main_done")
        sum_high = sem("sum_high")
        sum_high_dve = sem("sum_high_dve")
        sum_low = sem("sum_low")
        self_last = sem("self_last")
        self_ready = sem("self_ready")
        h_turned = sem("h_turned")
        h_copied = sem("h_copied")
        deg16_ready = sem("deg16_ready")
        deg_summed = sem("deg_summed")
        deg_clamped = sem("deg_clamped")
        rdeg_ready = sem("rdeg_ready")
        projected = sem("projected")
        out_read = sem("out_read")
        added = sem("added")
        x_again_full = [sem(f"x_again_full{n}") for n in range(2)]
        out_ready = sem("out_ready")
        stored = sem("stored")

        block = ctx.enter_context(nc.Block())

        def mask_words(n_slot):
            return mask[:, n_slot, :].bitcast(U32)

        def wait_lows(eng, e):
            by_vector = up_to(e, LOW_ON_VECTOR)
            by_pool = e + 1 - by_vector
            eng.wait_ge(low_pool, by_pool)
            if by_vector:
                eng.wait_ge(low_dve, by_vector)

        @block.sync
        def _(sp):
            def load_group(s, g):
                sub, a = divmod(g, QUAD)
                for q in range(QUAD):
                    sp.dma_start(stage[LANE * q:LANE * (q + 1), g % STAGES, :],
                                 adj_v[a, s, :, sub, q, :]).then_inc(stage_full[g % STAGES], DONE)

            def load_x(dst, s, q, signal):
                sp.dma_start(dst[LANE * q:LANE * (q + 1), :], x_v[q, s, :, :]).then_inc(signal, DONE)

            for e in range(CHUNKS):
                if e >= XRING:
                    wait_lows(sp, e - XRING)
                for q in range(QUAD):
                    load_x(x_ring[e % XRING].rearrange("p s d -> p (s d)"), e, q, x_full[e % XRING])
                if e == 3:
                    for dst, w in ((wc, w_comb), (ws, w_self), (wn, w_nb)):
                        sp.dma_start(dst, w.rearrange("(h p) n -> p h n", p=P)).then_inc(w_loaded, DONE)
                    sp.dma_start(bc_row, b_comb.rearrange("(a n) -> a n", a=1).partition_broadcast(P)
                                 ).then_inc(w_loaded, DONE)
                    for n, b in enumerate((b_self, b_nb)):
                        sp.dma_start(b_cols[:, n * HALVES:(n + 1) * HALVES], b.rearrange("(h p) -> p h", p=P),
                                     allow_slow_non_contiguous=True).then_inc(w_loaded, DONE)
                for g in GROUPS_OF_PAIR[e // 2] if e % 2 else []:
                    if g >= STAGES:
                        sp.wait_ge(masked, g - STAGES + 1)
                    load_group(0, g)

            def load_chunk(s, g0, g1):
                for g in range(g0, g1):
                    sp.wait_ge(masked, s * GROUPS + (g - STAGES + 1))
                    load_group(s, g)

            def reload_x(s, parity, first=False):
                if not first:
                    sp.wait_ge(stored, (s - 1) * (QUAD * DONE))
                for q in range(QUAD):
                    load_x(x_again[:, parity, :, :].rearrange("p s d -> p (s d)"), s, q, x_again_full[parity])

            def store(s, parity, sub0=0, subs=SUB):
                sp.wait_ge(out_ready, s * SUB + (sub0 + subs))
                for q in range(QUAD):
                    sp.dma_start(out_v[q, s, :, sub0 * D:(sub0 + subs) * D],
                                 x_again[LANE * q:LANE * (q + 1), parity, sub0:sub0 + subs, :]
                                 .rearrange("p s d -> p (s d)")).then_inc(stored, DONE)

            load_chunk(0, FIRST_GROUPS, GROUPS)
            load_chunk(1, 0, 4)
            wait_lows(sp, CHUNKS - 1)
            reload_x(0, 0, first=True)
            load_chunk(1, 4, 8)
            reload_x(1, 1, first=True)
            load_chunk(1, 8, GROUPS)

            def rest_of(s, parity, more=True):
                load_chunk(s, STAGES, GROUPS)
                store(s - 2, parity)
                if more:
                    load_chunk(s + 1, 0, STAGES)
                reload_x(s, parity)

            load_chunk(2, 0, STAGES)
            with sp.Fori(1, PAIRS) as k:
                for par in range(2):
                    rest_of(k * 2 + par, par)
            rest_of(CHUNKS - 2, 0)
            rest_of(CHUNKS - 1, 1, more=False)
            store(CHUNKS - 2, 0)
            store(CHUNKS - 1, 1, 0, SUB // 2)
            store(CHUNKS - 1, 1, SUB // 2, SUB // 2)
            sp.wait_ge(stored, (CHUNKS + 1) * QUAD * DONE)

        @block.gpsimd
        def _(pool):
            pool.memset(ident, 0.0).then_inc(zeroed, 1)
            pool.memset(ones, 1.0).then_inc(zeroed, 1)
            pool.memset(power, -0.5).then_inc(zeroed, 1)
            pool.memset(fold[:, :, :], 0.0).then_inc(zeroed, 1)
            pool.wait_ge(zeroed, 4)
            pool.affine_select(out=ident, in_=ident, compare_op=ALU.not_equal, fill=1.0, base=0,
                               pattern=[[-1, P]], channel_multiplier=1).then_inc(ident_ready, 1)

            def rstd_of(pair):
                two = slice(2 * pair, 2 * pair + 2)
                pool.wait_ge(aggr_done, 2 * SUB * (pair + 1))
                pool.tensor_scalar(var_s, mean_var[:, two, :, 1], EPS, SCALE ** -2,
                                   ALU.add, ALU.mult).then_inc(var_ready, 1)
                pool.wait_ge(var_ready, pair + 1)
                pool.tensor_tensor(rstd[:, two, :], var_s, power, ALU.pow).then_inc(rstd_ready, 1)

            def remainder(e):
                pool.wait_ge(high_ready, e + 1)
                tiles = slice(SUB * e, SUB * (e + 1))
                pool.tensor_tensor(h16[:, 1, tiles, :], x_ring[e % XRING], h16[:, 0, tiles, :],
                                   ALU.subtract).then_inc(low_pool, 1)

            for pair in range(CHUNKS // 2 + 2):
                for e in (2 * pair - 4, 2 * pair - 3):
                    if e % 2 and 2 * pair < CHUNKS:
                        rstd_of(pair)
                    if e >= 0 and e not in LOW_ON_VECTOR:
                        remainder(e)

        @block.scalar
        def _(act):
            def count(s, g, parity):
                act.wait_ge(masked, s * GROUPS + (g + 1))
                if not (isinstance(s, int) and s == 0 and g < 2):
                    act.wait_ge(counted_rows, s * GROUPS + (g - 1))
                act.activation(counted[:, g % 2, :], mask[:, g % MASKS, :], ACT.Copy,
                               accum_out=deg_part[:, parity, g:g + 1]).then_inc(counted_rows, 1)

            for e in range(CHUNKS):
                t = x_ring[e % XRING]
                if e in COUNTS_BEFORE:
                    count(0, COUNTS_BEFORE[e], 0)
                if e in NORM_ON_VECTOR:
                    act.wait_ge(normed, up_to(e, NORM_ON_VECTOR) * SUB)
                else:
                    act.wait_ge(shift_ready, e // 2 + 1)
                    for sub in range(SUB):
                        act.activation(t[:, sub, :], t[:, sub, :], ACT.Relu, bias=shift[:, e, sub:sub + 1],
                                       scale=rstd[:, e, sub:sub + 1]).then_inc(clipped, 1)
                    act.wait_ge(clipped, (e + 1 - up_to(e, NORM_ON_VECTOR)) * SUB)
                act.activation(h16[:, 0, SUB * e:SUB * (e + 1), :], t, ACT.Relu).then_inc(high_ready, 1)
                if e == 0:
                    act.wait_ge(w_loaded, 6 * DONE)
                    act.wait_ge(zeroed, 4)
                    for j in range(2 * HALVES):
                        act.activation(b_wide[:, j, :], ones, ACT.Copy, scale=b_cols[:, j:j + 1]).then_inc(wide_ready, 1)
                if e == 1:
                    act.wait_ge(w_turned, 1)
                    act.activation(ws_t.rearrange("p m k -> p (m k)"), banks[4][:, :], ACT.Copy).then_inc(wt_ready, 1)
                    act.activation(wn_t.rearrange("p m k -> p (m k)"), banks[5][:, :], ACT.Copy).then_inc(wt_ready, 1)
            act.wait_ge(w_product, 1)
            for w, bank in ((w1, banks[6]), (w2, banks[7])):
                act.activation(w[:, 0, :, :].rearrange("p h n -> p (h n)"), bank[:, :], ACT.Copy, scale=W_SCALE
                               ).then_inc(w_high, 1)
            act.wait_ge(w_high, 2)
            act.activation(w2[:, 2, :, :], w2[:, 0, :, :], ACT.Copy, scale=HIGH_SCALE).then_inc(w_ready, 1)
            for g in range(len(COUNTS_BEFORE), GROUPS):
                count(0, g, 0)

            def chunk_counts(s, parity, g0=0, g1=GROUPS, wait=False):
                if wait:
                    act.wait_ge(deg16_ready, s - 1)
                for g in range(g0, g1):
                    count(s, g, parity)

            def drain_h(s):
                act.wait_ge(h_turned, s + 1)
                for half in range(HALVES):
                    act.activation(h_t[:, half, :, :], h_ps[half], ACT.Copy).then_inc(h_copied, 1)

            def drain_sum(s, parity, halves=range(HALVES)):
                act.wait_ge(main_done, s + 1)
                for half in halves:
                    act.activation(sum_t[:, half, 0, :], sum_ps[parity][half][:, :], ACT.Copy, scale=HIGH_SCALE
                                   ).then_inc(sum_high, 1)

            def drain(s, parity, first=False):
                if first:
                    wait_lows(act, CHUNKS - 1)
                else:
                    act.wait_ge(projected, s * SUB)
                drain_sum(s, parity)
                drain_h(s)

            chunk_counts(1, 1, 0, 4)
            drain(0, 0, first=True)
            chunk_counts(1, 1, 4)
            chunk_counts(2, 0, 0, 13, wait=True)
            drain(1, 1)
            chunk_counts(2, 0, 13)
            chunk_counts(3, 1, wait=True)
            with act.Fori(1, PAIRS) as k:
                for par in range(2):
                    drain(k * 2 + par, par)
                    chunk_counts(k * 2 + (2 + par), par, wait=True)
            drain(CHUNKS - 2, 0)
            act.wait_ge(projected, (CHUNKS - 1) * SUB)
            drain_h(CHUNKS - 1)
            drain_sum(CHUNKS - 1, 1, [0])

        @block.tensor
        def _(pe):
            pe.wait_ge(w_loaded, 6 * DONE)
            pe.wait_ge(ident_ready, 2)
            for w, bank in ((ws, banks[4]), (wn, banks[5])):
                for m in range(HALVES):
                    for kk in range(HALVES):
                        at = m * D + kk * P
                        mm = pe.transpose(bank[:, at:at + P], w[:, kk, m * P:(m + 1) * P], ident)
            mm.then_inc(w_turned, 1)
            pe.wait_ge(wt_ready, 2)
            for n, (w_t, bank) in enumerate(((ws_t, banks[6]), (wn_t, banks[7]))):
                for kk in range(HALVES):
                    for m in range(HALVES):
                        pe.matmul(bank[:, kk * D:(kk + 1) * D], w_t[:, m, kk * P:(kk + 1) * P],
                                  wc[:, n * HALVES + m, :], start=(m == 0), stop=(m == HALVES - 1))
            pe.wait_ge(wide_ready, 2 * HALVES)
            for m in range(2 * HALVES):
                mm = pe.matmul(banks[3][:, 0:D], b_wide[:, m, :], wc[:, m, :],
                               start=(m == 0), stop=(m == 2 * HALVES - 1))
            mm.then_inc(w_product, 1)

            def sum_step(parity, e, sub, rows=slice(0, ROWS)):
                words = mask_t[:, parity, e, :, :].rearrange("p g l -> p (g l)").bitcast(FP8)
                rhs = words.rearrange("p (i s) -> p i s", s=SUB)[:, rows, sub]
                for half in range(HALVES):
                    for part in range(2):
                        mm = pe.matmul(sum_ps[parity][half][:, rows],
                                       h16[:, part, SUB * e + sub, half * P:(half + 1) * P], rhs,
                                       start=(rows.start == 0 and e == 0 and sub == 0 and part == 0),
                                       stop=(rows.stop == ROWS and e == CHUNKS - 1 and sub == SUB - 1 and part == 1))
                return mm

            def turn_h(s, first=False):
                if not first:
                    pe.wait_ge(h_copied, s * HALVES)
                for half in range(HALVES):
                    for sub in range(SUB):
                        for part in range(2):
                            lhs = h16[:, part, bass.ds(s * SUB + sub, 1), half * P:(half + 1) * P]
                            mm = pe.transpose(h_ps[half][:, part, sub * P:(sub + 1) * P],
                                              lhs.rearrange("p o d -> p (o d)"), ident16[:, :])
                mm.then_inc(h_turned, 1)

            def sum_degrees(s, bank, first=False):
                if first:
                    pe.wait_ge(fold_ready, QUAD * QUAD)
                pe.wait_ge(deg16_ready, s + 1)
                for a in range(QUAD):
                    mm = pe.matmul(bank[:, 0:SUB], fold[:, a, :], deg16[:, a:GROUPS:QUAD],
                                   start=(a == 0), stop=(a == QUAD - 1))
                mm.then_inc(deg_summed, 1)

            SELF_TERMS = ((0, 0), (0, 1), (1, 0))
            NB_TERMS = ((0, 0), (0, 1), (1, 2))

            def product(dst, sub, src, w, terms, start=True, stop=True):
                steps = [(half, i, j) for half in range(HALVES) for i, j in terms]
                for at, (half, i, j) in enumerate(steps):
                    mm = pe.matmul(dst, src[:, half, i, sub * P:(sub + 1) * P], w[:, j, half, :],
                                   start=(start and at == 0), stop=(stop and at == len(steps) - 1))
                return mm

            def project(s, sub, first=False):
                if sub == 0:
                    pe.wait_ge(h_copied, s * HALVES + HALVES)
                    pe.wait_ge(sum_low, s * HALVES + HALVES)
                if not (first and sub < 2):
                    pe.wait_ge(out_read, s * SUB + (sub - 1))
                product(out_ps[sub % 2][:, 0, :], sub, h_t, w1, SELF_TERMS)
                mm = product(out_ps[sub % 2][:, 1, :], sub, sum_t, w2, NB_TERMS)
                mm.then_inc(projected, 1)

            def chunk(s, parity, before, parts=1, degrees=10, projections=(13, 21, 29, 37), first=False):
                if first:
                    pe.wait_ge(w_ready, 4)
                else:
                    pe.wait_ge(rdeg_ready, s - 1)
                if parts == 1:
                    pe.wait_ge(transposed, s * GROUPS + GROUPS)
                turn_h(before, first)
                for part in range(parts):
                    if parts > 1:
                        pe.wait_ge(transposed, s * GROUPS + (part + 1) * (GROUPS // parts))
                    rows = slice(part * (ROWS // parts), (part + 1) * (ROWS // parts))
                    for tile in range(TILES):
                        mm = sum_step(parity, tile // SUB, tile % SUB, rows)
                        at, rest = divmod(part * TILES + tile, parts)
                        if rest:
                            continue
                        if at == degrees:
                            pe.wait_ge(sum_low, before * HALVES + HALVES)
                            sum_degrees(before, sum_ps[1 - parity][0], first)
                        if at in projections:
                            project(before, projections.index(at), first)
                        if s is last:
                            ahead_of_last(at)
                mm.then_inc(main_done, 1)

            last = CHUNKS - 1

            def ahead_of_last(at):
                if at == 40:
                    turn_h(last)
                if at == 48:
                    sum_degrees(last, sum_ps[(last - 1) % 2][0])
                if at == 52:
                    pe.wait_ge(h_copied, (last + 1) * HALVES)
                    pe.wait_ge(out_read, last * SUB)
                    for sub in range(SUB):
                        mm = product(last_ps[sub][:, 0, :], sub, h_t, w1, SELF_TERMS)
                    mm.then_inc(self_last, 1)

            QUARTER = GROUPS // 4
            SECOND_QUARTER = (9, lambda e: 0 if e < 9 else min(e + 1, 4 * e - 34))

            def quarter(n, e):
                for sub in range(SUB):
                    mm = sum_step(0, e, sub, slice(n * P, (n + 1) * P))
                return mm

            pe.wait_ge(transposed, QUARTER)
            behind = 0
            for e in range(CHUNKS):
                wait_lows(pe, e)
                quarter(0, e)
                if e == SECOND_QUARTER[0]:
                    pe.wait_ge(transposed, 2 * QUARTER)
                while behind < SECOND_QUARTER[1](e):
                    quarter(1, behind)
                    behind += 1
            for n in range(2, 4):
                pe.wait_ge(transposed, (n + 1) * QUARTER)
                for e in range(CHUNKS):
                    mm = quarter(n, e)
            mm.then_inc(main_done, 1)

            chunk(1, 1, 0, parts=4, degrees=8, projections=(11, 15, 19, 23), first=True)
            chunk(2, 0, 1, parts=2, degrees=8, projections=(11, 15, 19, 23))
            with pe.Fori(1, PAIRS) as k:
                for par in (1, 0):
                    chunk(k * 2 + (2 - par), par, k * 2 + (1 - par))
            chunk(last, last % 2, last - 1)
            pe.wait_ge(sum_high, (last + 1) * HALVES - 1)
            pe.wait_ge(sum_high_dve, 1)
            for sub in range(SUB):
                product(last_ps[sub][:, 1, :], sub, sum_t, w2, NB_TERMS[:2], stop=False)
            pe.wait_ge(sum_low, (last + 1) * HALVES)
            for sub in range(SUB):
                product(last_ps[sub][:, 1, :], sub, sum_t, w2, NB_TERMS[2:], start=False).then_inc(projected, 1)

        @block.vector
        def _(dve):
            last = CHUNKS - 1

            def form_mask(s, g):
                dve.wait_ge(stage_full[g % STAGES],
                            (s * (GROUPS // STAGES) + (g // STAGES + 1)) * (QUAD * DONE))
                if not (isinstance(s, int) and s == 0 and g < MASKS):
                    dve.wait_ge(counted_rows, s * GROUPS + (g - MASKS + 1))
                    dve.wait_ge(transposed, s * GROUPS + (g - MASKS + 1))
                dve.tensor_scalar(mask[:, g % MASKS, :], stage[:, g % STAGES, :], 0.0, float(ONE_BYTE),
                                  ALU.is_gt, ALU.mult).then_inc(masked, 1)

            def turn_mask(s, g, parity):
                dve.wait_ge(masked, s * GROUPS + (g + 1))
                src = mask_words(g % MASKS).rearrange("p (c l) -> p c l", l=LANE)
                dve.transpose(mask_t[:, parity, :, g, :], src).then_inc(transposed, 1)

            def stats_of(e):
                dve.wait_ge(x_full[e % XRING], (e // XRING + 1) * QUAD * DONE)
                for sub in range(SUB):
                    dve.bn_stats(stats[:, e % 2, sub, :], x_ring[e % XRING][:, sub, :]).then_inc(stats_done, 1)
                dve.wait_ge(stats_done, (e + 1) * SUB)
                for sub in range(SUB):
                    dve.bn_aggr(mean_var[:, e, sub, :], stats[:, e % 2, sub, :]).then_inc(aggr_done, 1)

            def normalise(pair):
                dve.wait_ge(rstd_ready, pair + 1)
                dve.scalar_tensor_tensor(shift[:, 2 * pair:2 * pair + 2, :], mean_var[:, 2 * pair:2 * pair + 2, :, 0], -1.0,
                                         rstd[:, 2 * pair:2 * pair + 2, :], ALU.mult, ALU.mult).then_inc(shift_ready, 1)
                for e in (2 * pair, 2 * pair + 1):
                    for sub in range(SUB if e in NORM_ON_VECTOR else 0):
                        t = x_ring[e % XRING][:, sub, :]
                        dve.tensor_scalar(t, t, mean_var[:, e, sub, 0:1], rstd[:, e, sub:sub + 1],
                                          ALU.subtract, ALU.mult).then_inc(normed, 1)

            def remainder(e):
                dve.wait_ge(high_ready, e + 1)
                tiles = slice(SUB * e, SUB * (e + 1))
                flat = "p s d -> p (s d)"
                dve.scalar_tensor_tensor(h16[:, 1, tiles, :].rearrange(flat), x_ring[e % XRING].rearrange(flat), 0.0,
                                         h16[:, 0, tiles, :].rearrange(flat), ALU.max, ALU.subtract
                                         ).then_inc(low_dve, 1)

            def pack(s, parity, first=False):
                dve.wait_ge(counted_rows, s * GROUPS + GROUPS)
                if not first:
                    dve.wait_ge(deg_summed, s)
                dve.tensor_scalar(deg16[:, :], deg_part[:, parity, :], 1.0 / ONE_BYTE, None, ALU.mult).then_inc(deg16_ready, 1)

            def remainder_of_sum(s, parity):
                if isinstance(s, int) and s == last:
                    dve.wait_ge(sum_high_dve, 1)
                    dve.wait_ge(sum_high, (s + 1) * HALVES - 1)
                else:
                    dve.wait_ge(sum_high, (s + 1) * HALVES)
                for half in range(HALVES):
                    dve.scalar_tensor_tensor(sum_t[:, half, 1, :], sum_t[:, half, 0, :], -1.0 / HIGH_SCALE,
                                             sum_ps[parity][half][:, :], ALU.mult, ALU.add).then_inc(sum_low, 1)

            def invert_degrees(s, bank):
                dve.wait_ge(deg_summed, s + 1)
                dve.tensor_scalar(deg[:, :], bank[:, 0:SUB], 1.0, NB_SCALE, ALU.max, ALU.mult
                                  ).then_inc(deg_clamped, 1)
                dve.wait_ge(deg_clamped, s + 1)
                dve.reciprocal(rdeg[:, :], deg[:, :]).then_inc(rdeg_ready, 1)

            def finish(pair, parity, sub):
                s = pair * 2 + parity
                dve.wait_ge(projected, s * SUB + (sub + 1))
                if sub == 0:
                    dve.wait_ge(rdeg_ready, s + 1)
                    dve.wait_ge(x_again_full[parity], (pair + 1) * (QUAD * DONE))
                y = layer[:, sub % 2, :]
                xa = x_again[:, parity, sub, :]
                dve.scalar_tensor_tensor(y, out_ps[sub % 2][:, 1, :], rdeg[:, sub:sub + 1], c_row[:, :],
                                         ALU.mult, ALU.add).then_inc(added, 1)
                dve.wait_ge(added, s * SUB + (sub + 1))
                dve.scalar_tensor_tensor(y, out_ps[sub % 2][:, 0, :], 1.0 / SELF_SCALE, y,
                                         ALU.mult, ALU.add).then_inc(out_read, 1)
                dve.wait_ge(out_read, s * SUB + (sub + 1))
                dve.scalar_tensor_tensor(xa, y, 0.0, xa, ALU.max, ALU.add).then_inc(out_ready, 1)

            dve.wait_ge(ident_ready, 1)
            dve.tensor_copy(ident16[:, :], ident).then_inc(ident_ready, 1)
            for q in range(QUAD):
                rows = slice(LANE * q, LANE * (q + 1))
                for a in range(QUAD):
                    dve.tensor_copy(fold[rows, a, LANE * a:LANE * (a + 1)], ident[rows, rows]
                                    ).then_inc(fold_ready, 1)

            for pair in range(CHUNKS // 2 + 2):
                groups = MASKS_OF_PAIR[pair]
                if 2 * pair < CHUNKS:
                    stats_of(2 * pair)
                if 1 <= pair <= CHUNKS // 2:
                    normalise(pair - 1)
                if 2 * pair < CHUNKS:
                    stats_of(2 * pair + 1)
                for g in groups:
                    form_mask(0, g)
                for g in groups:
                    turn_mask(0, g, 0)
                for e in (2 * pair - 4, 2 * pair - 3):
                    if e >= 0 and e in LOW_ON_VECTOR:
                        remainder(e)
            for g in range(sum(map(len, MASKS_OF_PAIR)), GROUPS):
                form_mask(0, g)
                turn_mask(0, g, 0)

            dve.wait_ge(w_product, 1)
            dve.tensor_tensor(c_row[:, :], banks[3][:, 0:D], bc_row, ALU.add).then_inc(w_ready, 1)
            for n, (w, bank) in enumerate(((w1, banks[6]), (w2, banks[7]))):
                dve.wait_ge(w_high, n + 1)
                flat = "p h n -> p (h n)"
                dve.scalar_tensor_tensor(w[:, 1, :, :].rearrange(flat), bank[:, :], W_SCALE, w[:, 0, :, :].rearrange(flat),
                                         ALU.mult, ALU.subtract).then_inc(w_ready, 1)

            for g in range(GROUPS):
                form_mask(1, g)
                if g == 0:
                    wait_lows(dve, CHUNKS - 1)
                    dve.wait_ge(w_ready, 4)
                else:
                    turn_mask(1, g - 1, 1)
                if g == 5:
                    pack(0, 0, first=True)
                if g == 7:
                    remainder_of_sum(0, 0)
                if g == 9:
                    invert_degrees(0, sum_ps[0][0])
                if g in (10, 12, 14, 15):
                    finish(0, 0, (10, 12, 14, 15).index(g))
            turn_mask(1, GROUPS - 1, 1)

            for g in range(GROUPS):
                form_mask(2, g)
                if g == 0:
                    dve.wait_ge(main_done, 1)
                else:
                    turn_mask(2, g - 1, 0)
                if g == 7:
                    pack(1, 1)
                if g == 13:
                    remainder_of_sum(1, 1)
            turn_mask(2, GROUPS - 1, 0)

            for g in range(GROUPS):
                form_mask(3, g)
                if g == 0:
                    dve.wait_ge(main_done, 2)
                else:
                    turn_mask(3, g - 1, 1)
                if g == 1:
                    invert_degrees(1, sum_ps[1][0])
                if g == 3:
                    pack(2, 0)
                if g in (2, 4, 6, 8):
                    finish(0, 1, (g - 2) // 2)
            turn_mask(3, GROUPS - 1, 1)

            with dve.Fori(2, PAIRS + 1) as k:
                for par in range(2):
                    s = k * 2 + par
                    for g in range(GROUPS):
                        form_mask(s, g)
                        if g == 0:
                            dve.wait_ge(main_done, s - 1)
                        else:
                            turn_mask(s, g - 1, par)
                        if g == 2:
                            remainder_of_sum(s - 2, par)
                        if g == 4:
                            invert_degrees(s - 2, sum_ps[par][0])
                            pack(s - 1, 1 - par)
                        if g in (6, 8, 10, 12):
                            finish(k - 1, par, (g - 6) // 2)
                    turn_mask(s, GROUPS - 1, par)
            remainder_of_sum(last - 1, 0)
            invert_degrees(last - 1, sum_ps[0][0])
            pack(last, 1)
            for sub in range(SUB):
                finish(last // 2, 0, sub)

            invert_degrees(last, sum_ps[0][0])
            dve.wait_ge(self_last, 1)
            dve.wait_ge(main_done, last)
            for sub in range(SUB):
                dve.scalar_tensor_tensor(self_c[:, sub * D:(sub + 1) * D], last_ps[sub][:, 0, :], 1.0 / SELF_SCALE,
                                         c_row[:, :], ALU.mult, ALU.add).then_inc(self_ready, 1)
            dve.wait_ge(rdeg_ready, last + 1)
            dve.wait_ge(x_again_full[1], (last // 2 + 1) * (QUAD * DONE))
            dve.wait_ge(self_ready, SUB)
            dve.wait_ge(main_done, last + 1)
            dve.tensor_scalar(sum_t[:, 1, 0, :], sum_ps[1][1][:, :], HIGH_SCALE, None, ALU.mult
                              ).then_inc(sum_high_dve, 1)
            remainder_of_sum(last, 1)
            for sub in range(SUB):
                dve.wait_ge(projected, last * SUB + (sub + 1))
                y = layer[:, sub % 2, :]
                xa = x_again[:, 1, sub, :]
                dve.scalar_tensor_tensor(y, last_ps[sub][:, 1, :], rdeg[:, sub:sub + 1],
                                         self_c[:, sub * D:(sub + 1) * D], ALU.mult, ALU.add).then_inc(added, 1)
                dve.wait_ge(added, last * SUB + (sub + 1))
                dve.scalar_tensor_tensor(xa, y, 0.0, xa, ALU.max, ALU.add).then_inc(out_ready, 1)


_INS = ["x", "adj", "L0_gnn_W_self", "L0_gnn_b_self", "L0_gnn_W_nb", "L0_gnn_b_nb", "L0_gnn_W_comb", "L0_gnn_b_comb"]


def kernel(**inputs):
    import numpy as np
    import concourse.bacc as bacc
    from concourse.bass_utils import run_bass_kernel_spmd

    nc = bacc.Bacc("TRN2", target_bir_lowering=False, num_devices=1)
    arrays, args = {}, []
    for name in _INS:
        a = np.ascontiguousarray(inputs[name])
        arrays[f"in_{name}_dram"] = a
        args.append(nc.dram_tensor(f"in_{name}_dram", a.shape, mybir.dt.from_np(a.dtype), kind="ExternalInput").ap())
    shape = arrays["in_x_dram"].shape
    out = nc.dram_tensor("out_0_dram", shape, F32, kind="ExternalOutput").ap()
    graph_layer(nc, *args, out)
    r = run_bass_kernel_spmd(nc, [arrays], core_ids=[0])
    return r.results[0]["out_0_dram"]
```
